# Optimizing a Trainium2 kernel written in Bass

```python
import numpy as np
import jax
import jax.numpy as jnp

def _softmax(x, axis=-1):
    return jax.nn.softmax(x, axis=axis)

def _gelu(x):
    return jax.nn.gelu(x, approximate=True)

def _silu(x):
    return jax.nn.silu(x)

def _sigmoid(x):
    return jax.nn.sigmoid(x)

def _layernorm(x, axis=-1, eps=1e-05):
    m = jnp.mean(x, axis=axis, keepdims=True)
    v = jnp.var(x, axis=axis, keepdims=True)
    return (x - m) / jnp.sqrt(v + eps)

def _scatter_add(tgt, idx, src, axis=0):
    return tgt.at[idx].add(src)

def _segment_sum(src, seg, n):
    return jax.ops.segment_sum(src, seg, n)
kernel_name = 'mk_sandwich_d1_jaxref_r8_fd2ae2'

def setup_inputs(seed: int=0):
    np.random.seed(seed)
    _w = jnp.asarray

    def _L0_attn_setup():
        import math
        import jax, jax.numpy as jnp
        import numpy as np
        N_HEADS = 16
        NUM_BUCKETS = 32
        MAX_DISTANCE = 128
        ROTARY_BASE = 10000.0

        def rotate_half(x):
            x1, x2 = jnp.split(x, 2, axis=-1)
            return jnp.concatenate((-x2, x1), axis=-1)

        def rotary_freqs(T, dim):
            inv_freq = 1.0 / ROTARY_BASE ** (jnp.arange(0, dim, 2, dtype=jnp.float32) / dim)
            t = jnp.arange(T, dtype=jnp.float32)
            freqs = jnp.einsum('i,j->ij', t, inv_freq)
            return jnp.concatenate((freqs, freqs), axis=-1)

        def rel_pos_bucket_causal(rel_pos, num_buckets=NUM_BUCKETS, max_distance=MAX_DISTANCE):
            n = jnp.maximum(-rel_pos, 0)
            max_exact = num_buckets // 2
            is_small = n < max_exact
            n_safe = jnp.maximum(n, 1).astype(jnp.float32)
            val_if_large = max_exact + (jnp.log(n_safe / max_exact) / math.log(max_distance / max_exact) * (num_buckets - max_exact)).astype(jnp.int32)
            val_if_large = jnp.minimum(val_if_large, num_buckets - 1)
            return jnp.where(is_small, n, val_if_large)
        key = jax.random.key(seed)
        ks = jax.random.split(key, 10)
        B, T, C = (2, 256, 128)
        s = 0.02
        return {'x': jax.random.normal(ks[0], (B, T, C), dtype=jnp.float32), 'Wq': jax.random.normal(ks[1], (C, C), dtype=jnp.float32) * s, 'bq': jnp.zeros((C,), dtype=jnp.float32), 'Wk': jax.random.normal(ks[2], (C, C), dtype=jnp.float32) * s, 'bk': jnp.zeros((C,), dtype=jnp.float32), 'Wv': jax.random.normal(ks[3], (C, C), dtype=jnp.float32) * s, 'bv': jnp.zeros((C,), dtype=jnp.float32), 'Wp': jax.random.normal(ks[4], (C, C), dtype=jnp.float32) * s, 'bp': jnp.zeros((C,), dtype=jnp.float32), 'rel_bias_table': jax.random.normal(ks[5], (NUM_BUCKETS, N_HEADS), dtype=jnp.float32) * s}
    _L0_attn_in = _L0_attn_setup()

    def _L0_ffn_setup():
        import jax, jax.numpy as jnp
        import numpy as np
        EMB = 128
        HID = 256
        HEADS = 16
        HEAD_DIM = EMB // HEADS
        EXPERTS = 8
        TOPK = 2
        EPS = 1e-05

        def layernorm(x, scale, shift):
            mean = jnp.mean(x, axis=-1, keepdims=True)
            var = jnp.mean((x - mean) ** 2, axis=-1, keepdims=True)
            return scale * (x - mean) / jnp.sqrt(var + EPS) + shift

        def attention(x, wq, wk, wv, wo, bo):
            b, t, _ = x.shape
            q = (x @ wq).reshape(b, t, HEADS, HEAD_DIM)
            k = (x @ wk).reshape(b, t, HEADS, HEAD_DIM)
            v = (x @ wv).reshape(b, t, HEADS, HEAD_DIM)
            scores = jnp.einsum('bqhd,bkhd->bhqk', q, k)
            mask = jnp.arange(t)[:, None] < jnp.arange(t)[None, :]
            scores = jnp.where(mask, -jnp.inf, scores)
            attn = jax.nn.softmax(scores / np.sqrt(HEAD_DIM), axis=-1)
            ctx = jnp.einsum('bhqk,bkhd->bqhd', attn, v).reshape(b, t, EMB)
            return ctx @ wo + bo

        def moe_ff(x, gate_w, w1, w2, w3):
            b, t, d = x.shape
            xf = x.reshape(b * t, d)
            scores = xf @ gate_w
            topk_scores, topk_idx = jax.lax.top_k(scores, TOPK)
            topk_probs = jax.nn.softmax(topk_scores, axis=-1)
            weight = jnp.sum(jax.nn.one_hot(topk_idx, EXPERTS, dtype=xf.dtype) * topk_probs[..., None], axis=1)
            h = jax.nn.silu(jnp.einsum('td,edh->eth', xf, w1)) * jnp.einsum('td,edh->eth', xf, w2)
            out_e = jnp.einsum('eth,ehd->etd', h, w3)
            out = jnp.einsum('etd,te->td', out_e, weight)
            return out.reshape(b, t, d)
        key = jax.random.key(seed)
        ks = jax.random.split(key, 12)
        s = lambda k, shape, fan: jax.random.normal(k, shape, jnp.float32) / np.sqrt(fan)
        return {'x': jax.random.normal(ks[0], (2, 256, EMB), jnp.float32), 'ln1_scale': jnp.ones((EMB,), jnp.float32), 'ln1_shift': jnp.zeros((EMB,), jnp.float32), 'wq': s(ks[1], (EMB, EMB), EMB), 'wk': s(ks[2], (EMB, EMB), EMB), 'wv': s(ks[3], (EMB, EMB), EMB), 'wo': s(ks[4], (EMB, EMB), EMB), 'bo': jnp.zeros((EMB,), jnp.float32), 'ln2_scale': jnp.ones((EMB,), jnp.float32), 'ln2_shift': jnp.zeros((EMB,), jnp.float32), 'gate_w': s(ks[5], (EMB, EXPERTS), EMB), 'w1': s(ks[6], (EXPERTS, EMB, HID), EMB), 'w2': s(ks[7], (EXPERTS, EMB, HID), EMB), 'w3': s(ks[8], (EXPERTS, HID, EMB), HID)}
    _L0_ffn_in = _L0_ffn_setup()
    _d = {'L0_attn_x': _L0_attn_in['x'], 'L0_attn_Wq': _L0_attn_in['Wq'], 'L0_attn_bq': _L0_attn_in['bq'], 'L0_attn_Wk': _L0_attn_in['Wk'], 'L0_attn_bk': _L0_attn_in['bk'], 'L0_attn_Wv': _L0_attn_in['Wv'], 'L0_attn_bv': _L0_attn_in['bv'], 'L0_attn_Wp': _L0_attn_in['Wp'], 'L0_attn_bp': _L0_attn_in['bp'], 'L0_attn_rel_bias_table': _L0_attn_in['rel_bias_table'], 'L0_ffn_ln1_scale': _L0_ffn_in['ln1_scale'], 'L0_ffn_ln1_shift': _L0_ffn_in['ln1_shift'], 'L0_ffn_wq': _L0_ffn_in['wq'], 'L0_ffn_wk': _L0_ffn_in['wk'], 'L0_ffn_wv': _L0_ffn_in['wv'], 'L0_ffn_wo': _L0_ffn_in['wo'], 'L0_ffn_bo': _L0_ffn_in['bo'], 'L0_ffn_ln2_scale': _L0_ffn_in['ln2_scale'], 'L0_ffn_ln2_shift': _L0_ffn_in['ln2_shift'], 'L0_ffn_gate_w': _L0_ffn_in['gate_w'], 'L0_ffn_w1': _L0_ffn_in['w1'], 'L0_ffn_w2': _L0_ffn_in['w2'], 'L0_ffn_w3': _L0_ffn_in['w3']}
    _x0 = _d['L0_attn_x']
    _d['L0_attn_x'] = jax.random.normal(jax.random.fold_in(jax.random.key(seed), 1), (16, 512, 128), dtype=_x0.dtype)
    del _x0
    return _d

def reference(L0_attn_x, L0_attn_Wq, L0_attn_bq, L0_attn_Wk, L0_attn_bk, L0_attn_Wv, L0_attn_bv, L0_attn_Wp, L0_attn_bp, L0_attn_rel_bias_table, L0_ffn_ln1_scale, L0_ffn_ln1_shift, L0_ffn_wq, L0_ffn_wk, L0_ffn_wv, L0_ffn_wo, L0_ffn_bo, L0_ffn_ln2_scale, L0_ffn_ln2_shift, L0_ffn_gate_w, L0_ffn_w1, L0_ffn_w2, L0_ffn_w3):

    def _L0_attn_ref(x, Wq, bq, Wk, bk, Wv, bv, Wp, bp, rel_bias_table):
        import math
        import jax, jax.numpy as jnp
        import numpy as np
        N_HEADS = 16
        NUM_BUCKETS = 32
        MAX_DISTANCE = 128
        ROTARY_BASE = 10000.0

        def rotate_half(x):
            x1, x2 = jnp.split(x, 2, axis=-1)
            return jnp.concatenate((-x2, x1), axis=-1)

        def rotary_freqs(T, dim):
            inv_freq = 1.0 / ROTARY_BASE ** (jnp.arange(0, dim, 2, dtype=jnp.float32) / dim)
            t = jnp.arange(T, dtype=jnp.float32)
            freqs = jnp.einsum('i,j->ij', t, inv_freq)
            return jnp.concatenate((freqs, freqs), axis=-1)

        def rel_pos_bucket_causal(rel_pos, num_buckets=NUM_BUCKETS, max_distance=MAX_DISTANCE):
            n = jnp.maximum(-rel_pos, 0)
            max_exact = num_buckets // 2
            is_small = n < max_exact
            n_safe = jnp.maximum(n, 1).astype(jnp.float32)
            val_if_large = max_exact + (jnp.log(n_safe / max_exact) / math.log(max_distance / max_exact) * (num_buckets - max_exact)).astype(jnp.int32)
            val_if_large = jnp.minimum(val_if_large, num_buckets - 1)
            return jnp.where(is_small, n, val_if_large)
        B, T, C = x.shape
        H = N_HEADS
        D = C // H

        def heads(y):
            return y.reshape(B, T, H, D).transpose(0, 2, 1, 3)
        q = heads(x @ Wq + bq)
        k = heads(x @ Wk + bk)
        v = heads(x @ Wv + bv)
        freqs = rotary_freqs(T, D)
        cos, sin = (jnp.cos(freqs), jnp.sin(freqs))
        q = q * cos + rotate_half(q) * sin
        k = k * cos + rotate_half(k) * sin
        pos = jnp.arange(T)
        rel_pos = pos[None, :] - pos[:, None]
        bucket = rel_pos_bucket_causal(rel_pos)
        bias = rel_bias_table[bucket]
        bias = bias.transpose(2, 0, 1)
        att = jnp.einsum('bhid,bhjd->bhij', q, k) + bias[None]
        att = att * (1.0 / math.sqrt(D))
        causal = pos[None, :] <= pos[:, None]
        att = jnp.where(causal[None, None], att, -jnp.inf)
        att = jax.nn.softmax(att, axis=-1)
        y = jnp.einsum('bhij,bhjd->bhid', att, v)
        y = y.transpose(0, 2, 1, 3).reshape(B, T, C)
        return y @ Wp + bp

    def _L0_ffn_ref(x, ln1_scale, ln1_shift, wq, wk, wv, wo, bo, ln2_scale, ln2_shift, gate_w, w1, w2, w3):
        import jax, jax.numpy as jnp
        import numpy as np
        EMB = 128
        HID = 256
        HEADS = 16
        HEAD_DIM = EMB // HEADS
        EXPERTS = 8
        TOPK = 2
        EPS = 1e-05

        def layernorm(x, scale, shift):
            mean = jnp.mean(x, axis=-1, keepdims=True)
            var = jnp.mean((x - mean) ** 2, axis=-1, keepdims=True)
            return scale * (x - mean) / jnp.sqrt(var + EPS) + shift

        def attention(x, wq, wk, wv, wo, bo):
            b, t, _ = x.shape
            q = (x @ wq).reshape(b, t, HEADS, HEAD_DIM)
            k = (x @ wk).reshape(b, t, HEADS, HEAD_DIM)
            v = (x @ wv).reshape(b, t, HEADS, HEAD_DIM)
            scores = jnp.einsum('bqhd,bkhd->bhqk', q, k)
            mask = jnp.arange(t)[:, None] < jnp.arange(t)[None, :]
            scores = jnp.where(mask, -jnp.inf, scores)
            attn = jax.nn.softmax(scores / np.sqrt(HEAD_DIM), axis=-1)
            ctx = jnp.einsum('bhqk,bkhd->bqhd', attn, v).reshape(b, t, EMB)
            return ctx @ wo + bo

        def moe_ff(x, gate_w, w1, w2, w3):
            b, t, d = x.shape
            xf = x.reshape(b * t, d)
            scores = xf @ gate_w
            topk_scores, topk_idx = jax.lax.top_k(scores, TOPK)
            topk_probs = jax.nn.softmax(topk_scores, axis=-1)
            weight = jnp.sum(jax.nn.one_hot(topk_idx, EXPERTS, dtype=xf.dtype) * topk_probs[..., None], axis=1)
            h = jax.nn.silu(jnp.einsum('td,edh->eth', xf, w1)) * jnp.einsum('td,edh->eth', xf, w2)
            out_e = jnp.einsum('eth,ehd->etd', h, w3)
            out = jnp.einsum('etd,te->td', out_e, weight)
            return out.reshape(b, t, d)
        h = layernorm(x, ln1_scale, ln1_shift)
        x = x + attention(h, wq, wk, wv, wo, bo)
        h = layernorm(x, ln2_scale, ln2_shift)
        x = x + moe_ff(h, gate_w, w1, w2, w3)
        return x
    x = L0_attn_x
    x = x + _layernorm(_L0_attn_ref(_layernorm(x, axis=-1), L0_attn_Wq, L0_attn_bq, L0_attn_Wk, L0_attn_bk, L0_attn_Wv, L0_attn_bv, L0_attn_Wp, L0_attn_bp, L0_attn_rel_bias_table), axis=-1)
    x = x + _layernorm(_L0_ffn_ref(_layernorm(x, axis=-1), L0_ffn_ln1_scale, L0_ffn_ln1_shift, L0_ffn_wq, L0_ffn_wk, L0_ffn_wv, L0_ffn_wo, L0_ffn_bo, L0_ffn_ln2_scale, L0_ffn_ln2_shift, L0_ffn_gate_w, L0_ffn_w1, L0_ffn_w2, L0_ffn_w3), axis=-1)
    return x

_drawn_inputs = setup_inputs


def setup_inputs(seed=0):
    import zlib

    import numpy as np

    out = dict(_drawn_inputs(seed))
    spreads = {'L0_attn_bq': (0.0, 0.8),
     'L0_attn_bk': (0.0, 0.8),
     'L0_attn_bv': (0.0, 0.1),
     'L0_attn_bp': (0.0, 0.1),
     'L0_ffn_ln1_scale': (1.0, 0.2),
     'L0_ffn_ln1_shift': (0.0, 0.1),
     'L0_ffn_bo': (0.0, 0.1),
     'L0_ffn_ln2_scale': (1.0, 0.2),
     'L0_ffn_ln2_shift': (0.0, 0.1)}
    factors = {'L0_attn_Wq': 8.0, 'L0_attn_Wk': 8.0, 'L0_attn_rel_bias_table': 64.0}
    for name, (base, spread) in spreads.items():
        noise = np.random.default_rng([zlib.crc32(name.encode()), seed]).standard_normal(out[name].shape)
        drawn = base * np.exp(spread * noise) if base else spread * noise
        out[name] = jnp.asarray(drawn.astype(out[name].dtype))
    for name, factor in factors.items():
        out[name] = (out[name] * factor).astype(out[name].dtype)
    return out
```

```python
from contextlib import ExitStack

import numpy as np

import concourse.bass as bass
from concourse import mybir

F32 = mybir.dt.float32
BF16 = mybir.dt.bfloat16
U32 = mybir.dt.uint32
ALU = mybir.AluOpType
ACT = mybir.ActivationFunctionType
AX_X = mybir.AxisListType.X

B, T, C = 16, 512, 128
H = 16
D = C // H
P = 128
NT = T // P
PAIRS = H // 2
GROUPS = 4
GH = H // GROUPS
GP = GH // 2
SCALE = float(1.0 / np.sqrt(D))
EPS = 1e-5
SLOTS = 6
ROWS = SLOTS * D
MROWS = 3
BUCKETS = 32
BAND = 384
NEAR = 2 * P
MASKED = -1e30
EXPERTS, HID = 8, 256
HALVES = HID // P
VCOL = 32
NORMS = 6
RING = 3
PBUF = 3
EBUF = 3
NBUF = 4

MAX_PIECES = [(0, 0, 2), (1, 0, 2), (2, 0, 1), (2, 1, 1), (3, 0, 1), (3, 1, 1)]
EXP_PIECES = [(0, 0, 1), (0, 1, 1), (1, 0, 1), (1, 1, 1), (2, 0, 2), (3, 0, 2)]


def attention_schedule():
    order = []

    def exps(g):
        out = []
        for i in range(len(EXP_PIECES)):
            out.append([("E", g, i)])
            kt = {2: 0, 4: 1, 5: 2}.get(i)
            if kt is not None:
                out[-1].append(("V", g, kt))
        return out

    order += [("M", 0, i) for i in range(6)]
    order += [("M", 1, i) for i in range(3)] + [("T", 0, 0)] + [("M", 1, i) for i in range(3, 6)]
    for g in range(GROUPS):
        for i, steps in enumerate(exps(g)):
            if g + 2 < GROUPS:
                order.append(("M", g + 2, i))
            order += steps
            if i == 0 and g:
                order.append(("V", g - 1, 3))
            if i == 1 and g + 1 < GROUPS:
                order.append(("T", g + 1, 0))
    order.append(("V", GROUPS - 1, 3))
    return order


SCHEDULE = attention_schedule()
RING_USES = [s for s in SCHEDULE if s[0] != "V"]
V_USES = [s for s in SCHEDULE if s[0] == "V"]
DONE_BY = {"M": [s for s in RING_USES if s[0] == "M"], "E": [s for s in RING_USES if s[0] == "E"],
           "T": [s for s in RING_USES if s[0] == "T"]}


def nth(kind, g, i):
    return (V_USES if kind == "V" else DONE_BY[kind]).index((kind, g, i)) + 1


def ring_slot(step):
    return RING_USES.index(step) % RING


def shape_constants():
    inv = 1.0 / 10000.0 ** (np.arange(0, D, 2, dtype=np.float32) / D)
    freqs = np.arange(T, dtype=np.float32)[:, None] * inv[None, :].astype(np.float32)
    freqs = np.concatenate([freqs, freqs], axis=-1)
    cos, sin = np.cos(freqs).T, np.sin(freqs).T
    sign = np.where(np.arange(D) < D // 2, -1.0, 1.0)[:, None]
    spread = lambda x: np.broadcast_to(x[None, :, None, :], (2, D, PAIRS, T)).reshape(P, T)
    n = np.arange(BAND) - (P - 1)
    exact = BUCKETS // 2
    far = exact + (np.log(np.maximum(n, 1).astype(np.float32) / exact) / np.log(128 / exact)
                   * (BUCKETS - exact)).astype(np.int32)
    bucket = np.where(n < exact, n, np.minimum(far, BUCKETS - 1))
    bucket = np.where(n < 0, BUCKETS, bucket)
    forward = (np.arange(BUCKETS + 1)[:, None] == bucket[None, :])
    mirrored_n = (NEAR - 1) - np.arange(BAND)
    backward = np.zeros((BUCKETS + 1, BAND), bool)
    for m in range(BAND - 1):
        backward[:, m] = forward[:, mirrored_n[m] + P - 1]
    eye = np.eye(P)
    causal = np.where(np.arange(P)[:, None] > np.arange(P)[None, :], MASKED, 0.0)
    experts = np.zeros((3, EXPERTS, EXPERTS, P))
    for e in range(EXPERTS):
        experts[:, e, e, :] = 1.0
    f = lambda x: np.ascontiguousarray(x, dtype=np.float32)
    return {
        "cos": f(spread(cos)), "sin": f(spread(sin * sign)),
        "band": f(np.stack([forward, backward], axis=1)),
        "eye": f(eye),
        "mask_kq": f(causal), "mask_qk": f(causal.T),
        "expert_rows": f(experts.reshape(3 * EXPERTS, EXPERTS * P)),
        "expert_ids": f(np.broadcast_to(np.arange(EXPERTS), (P, NT, EXPERTS))),
    }


def sandwich(nc, din, const, out):
    ctx = ExitStack()
    with ctx:
        def sb(name, shape, dt=F32):
            return ctx.enter_context(nc.sbuf_tensor(name, shape, dt))

        sems = []

        def sem(name):
            s = ctx.enter_context(nc.semaphore(name))
            sems.append(s)
            return s

        def sem2(name):
            return [sem(f"{name}{i}") for i in range(2)]

        def scratch(name, shape, dt):
            return nc.dram_tensor(name, shape, dt, kind="Internal").ap()

        q_bounce = [scratch(f"q_bounce{i}", [2, ROWS, PAIRS * T], BF16) for i in range(2)]
        k_bounce = [scratch(f"k_bounce{i}", [2, ROWS, PAIRS * T], BF16) for i in range(2)]
        m_bounce = [scratch(f"m_bounce{i}", [GROUPS, 2, MROWS, GP * T], BF16) for i in range(2)]
        band_bounce = scratch("band_bounce", [2, P, H, BAND], F32)

        cos_t, sin_t = sb("cos_t", [P, T]), sb("sin_t", [P, T])
        eye = sb("eye", [P, P])
        eye_bf = sb("eye_bf", [P, P], BF16)
        mask_f = sb("mask_f", [P, 2, P])
        mask_kq, mask_qk = sb("mask_kq", [P, P], BF16), sb("mask_qk", [P, P], BF16)
        onehot = sb("onehot", [BUCKETS + 1, 2, BAND])
        table = sb("table", [BUCKETS + 1, H])
        table_far = sb("table_far", [BUCKETS, H])
        band = sb("band", [H, 2, BAND])
        bias_qk = sb("bias_qk", [P, H, NEAR])
        bias_kq = sb("bias_kq", [P, 3, H, NEAR], BF16)
        expert_rows_f = sb("expert_rows_f", [3 * EXPERTS, EXPERTS * P])
        expert_rows = sb("expert_rows", [3 * EXPERTS, EXPERTS * P], BF16)
        expert_ids = sb("expert_ids", [P, NT, EXPERTS])
        wq = [sb(f"wq{i}", [P, C]) for i in range(2)]
        wk = [sb(f"wk{i}", [P, C]) for i in range(2)]
        wv = [sb(f"wv{i}", [P, C]) for i in range(2)]
        wo = [sb(f"wo{i}", [P, C]) for i in range(2)]
        wq_rot, wk_rot = sb("wq_rot", [P, C]), sb("wk_rot", [P, C])
        bias_cols = sb("bias_cols", [P, 4])
        ln_cols = sb("ln_cols", [P, 4])
        bv_row, bo_row = sb("bv_row", [P, C]), [sb(f"bo_row{i}", [P, C]) for i in range(2)]
        gate = sb("gate", [P, EXPERTS])
        w1, w2 = sb("w1", [P, EXPERTS, HID]), sb("w2", [P, EXPERTS, HID])
        w3 = sb("w3", [P, EXPERTS, HALVES, C])
        minus_half = sb("minus_half", [P, NT])

        x = sb("x", [P, NT, C])
        resid = [sb(f"resid{i}", [P, NT, C]) for i in range(4)]
        normed = [sb(f"normed{i}", [P, NT, C]) for i in range(2)]
        stats = sb("stats", [P, NT, 6])
        mean_var = sb("mean_var", [P, NORMS, NT, 2])
        var_eps = sb("var_eps", [P, NORMS, NT])
        rstd = sb("rstd", [P, NORMS, NT])
        hT = sb("hT", [P, T])
        rope_a, rope_b = sb("rope_a", [P, 2, T]), sb("rope_b", [P, 2, T])
        qk_f = sb("qk_f", [P, 2, T])
        qk_rest = sb("qk_rest", [P, 2, T])
        q_parts, k_parts = sb("q_parts", [P, 3, T], BF16), sb("k_parts", [P, 3, T], BF16)
        q_stack, k_stack = sb("q_stack", [P, PAIRS, T], BF16), sb("k_stack", [P, PAIRS, T], BF16)
        v_aug = sb("v_aug", [P, NT, H, VCOL])
        near_sum = sb("near_sum", [P, NBUF, NEAR])
        near_max, far_max = sb("near_max", [P, NT, H]), sb("far_max", [P, NT, H])
        neg_max = sb("neg_max", [P, GROUPS, NT, GH])
        m_rest = sb("m_rest", [P, GROUPS, NT, GH])
        m_rest2 = sb("m_rest2", [P, GROUPS, NT, GH])
        m_parts = sb("m_parts", [P, GROUPS, NT, 2, MROWS, GP], BF16)
        m_rows = sb("m_rows", [2 * MROWS * GP, 2, T], BF16)
        probs = sb("probs", [P, PBUF, GH, T])
        ctxT = sb("ctxT", [P, GROUPS, T])
        row_inv = sb("row_inv", [P, NT, H])
        ctx_tok = sb("ctx_tok", [P, NT, C])
        ctx_ch = sb("ctx_ch", [P, T])
        gate_s = sb("gate_s", [P, NT, EXPERTS])
        top8 = sb("top8", [P, NT, EXPERTS])
        top_ids = sb("top_ids", [P, NT, EXPERTS], U32)
        top_ids_f = sb("top_ids_f", [P, NT, 2])
        gap = sb("gap", [P, NT])
        gap_exp = sb("gap_exp", [P, NT])
        gap_den = sb("gap_den", [P, NT])
        top_p = sb("top_p", [P, 2, NT])
        pick = sb("pick", [P, 2, NT, EXPERTS])
        pick_w = sb("pick_w", [P, 2, NT, EXPERTS])
        weight = sb("weight", [P, NT, EXPERTS])
        weight_rest = sb("weight_rest", [P, 2, NT, EXPERTS])
        weight_parts = sb("weight_parts", [P, NT, 3, EXPERTS], BF16)
        weight_rows = sb("weight_rows", [3 * EXPERTS, T], BF16)
        weight_bc = sb("weight_bc", [P, 2, T])
        spare = probs[:, :, :, :].rearrange("p a b n -> p (a b) n")
        tanh_t, gated, hidden, hidden_w = (spare[:, EBUF * i:EBUF * (i + 1), :] for i in range(4))
        moe_ch = sb("moe_ch", [P, T])
        result = sb("result", [P, NT, C])

        ring = [ctx.enter_context(nc.psum_tensor(f"ring{i}", [P, 2, T], F32)) for i in range(RING)]
        single = [ctx.enter_context(nc.psum_tensor(f"single{i}", [P, T], F32)) for i in range(2)]

        def bank(i):
            return ring[i // 2][:, i % 2, :]

        loaded, setup_step, setup_mm = sem("loaded"), sem("setup_step"), sem("setup_mm")
        band_written, band_read = sem("band_written"), sem("band_read")
        x_loaded = sem("x_loaded")
        vector_step, pool_step = sem("vector_step"), sem("pool_step")
        var_ready, rstd_ready = sem("var_ready"), sem("rstd_ready")
        normed_ready, normedT_ready, hT_ready = sem("normed_ready"), sem("normedT_ready"), sem("hT_ready")
        qk_proj, v_proj = sem2("qk_proj"), sem2("v_proj")
        qk_copied, rope_ready = sem("qk_copied"), sem("rope_ready")
        q_split, k_split, v_ready = sem2("q_split"), sem2("k_split"), sem2("v_ready")
        q_bounced, k_bounced, q_rows, k_rows = (sem2(n) for n in ("q_bounced", "k_bounced", "q_rows", "k_rows"))
        max_scores, max_done = sem2("max_scores"), sem2("max_done")
        group_max, m_split = sem2("group_max"), sem2("m_split")
        m_turned, m_copied = sem2("m_turned"), sem2("m_copied")
        m_bounced = [[sem(f"m_bounced{i}_{g}") for g in range(GROUPS)] for i in range(2)]
        m_in_stack = [[sem(f"m_in_stack{i}_{g}") for g in range(GROUPS)] for i in range(2)]
        exp_scores, exp_done = sem2("exp_scores"), sem2("exp_done")
        values_done, ctxT_copied = sem2("values_done"), sem2("ctxT_copied")
        ctx_turned, ctx_ready = sem2("ctx_turned"), sem2("ctx_ready")
        ctx_back, ctx_copied, y_ready = sem2("ctx_back"), sem2("ctx_copied"), sem2("y_ready")
        near_added = sem("near_added")
        gate_ready, gap_ready, gap_exp_ready = sem("gate_ready"), sem("gap_ready"), sem("gap_exp_ready")
        weight_split, weight_turned, weight_copied = sem("weight_split"), sem("weight_turned"), sem("weight_copied")
        weight_wide, weight_bc_ready = sem("weight_wide"), sem("weight_bc_ready")
        up_ready, tanh_ready, gated_ready = sem("up_ready"), sem("tanh_ready"), sem("gated_ready")
        hidden_ready, hidden_w_ready = sem("hidden_ready"), sem("hidden_w_ready")
        down_done, moe_ready, moe_copied, moe_turned = sem("down_done"), sem("moe_ready"), sem("moe_copied"), sem("moe_turned")
        result_ready, stored = sem("result_ready"), sem("stored")
        all_sems = range(min(s.num for s in sems), max(s.num for s in sems) + 1)

        n_loads = [0]
        with nc.Block() as block:
            def load(eng, dst, src):
                n_loads[0] += 1
                eng.dma_start(dst, src).then_inc(loaded, 16)

            def across(name):
                v = din[name]
                return bass.AP(tensor=v.tensor, offset=v.offset, ap=[[0, P], [1, C]])

            @block.sync
            def _(sp):
                load(sp, onehot[:, :, :], const["band"])
                load(sp, table[0:BUCKETS, :], din["L0_attn_rel_bias_table"])
                tb = din["L0_attn_rel_bias_table"]
                load(sp, table_far[:, :], bass.AP(tensor=tb.tensor, offset=tb.offset + (BUCKETS - 1) * H,
                                                  ap=[[0, BUCKETS], [1, H]]))
                load(sp, cos_t[:, :], const["cos"])
                load(sp, sin_t[:, :], const["sin"])
                load(sp, eye[:, :], const["eye"])
                load(sp, mask_f[:, 0, :], const["mask_kq"])
                load(sp, mask_f[:, 1, :], const["mask_qk"])
                load(sp, expert_rows_f[:, :], const["expert_rows"])
                load(sp, expert_ids[:, :, :], const["expert_ids"])
                for i, w in enumerate((wq[0], wk[0], wq[1], wk[1], wq_rot, wk_rot)):
                    load(sp, w[:, :], din["qk_weights"][i])
                load(sp, bias_cols[:, :], din["qk_biases"])
                load(sp, wv[0][:, :], din["L0_attn_Wv"])
                load(sp, wv[1][:, :], din["L0_ffn_wv"])
                load(sp, wo[0][:, :], din["L0_attn_Wp"])
                load(sp, wo[1][:, :], din["L0_ffn_wo"])
                for i, n in enumerate(("ln1_scale", "ln1_shift", "ln2_scale", "ln2_shift")):
                    load(sp, ln_cols[:, i:i + 1], din["L0_ffn_" + n].rearrange("(c a) -> c a", a=1))
                load(sp, bv_row[:, :], across("L0_attn_bv"))
                load(sp, bo_row[0][:, :], across("L0_attn_bp"))
                load(sp, bo_row[1][:, :], across("L0_ffn_bo"))
                load(sp, gate[:, :], din["L0_ffn_gate_w"])
                load(sp, w1[:, :, :], din["L0_ffn_w1"].rearrange("e c h -> c e h"))
                load(sp, w2[:, :, :], din["L0_ffn_w2"].rearrange("e c h -> c e h"))
                load(sp, w3[:, :, :, :].rearrange("c e a d -> c (e a) d"),
                     din["L0_ffn_w3"].rearrange("e (a c) d -> c (e a) d", a=HALVES))
                sp.wait_ge(setup_step, 5)
                for v in range(2):
                    sp.dma_start(band_bounce[v].rearrange("r h m -> h r m"),
                                 band[:, v, :].unsqueeze(1).broadcast_to([H, P, BAND])).then_inc(band_written, 16)
                sp.wait_ge(band_written, 32)
                pitch = H * BAND
                for v, dst in ((0, probs[:, 0:2, :, :].rearrange("p a b c -> p (a b c)").rearrange("p (h m) -> p h m", h=H)), (1, bias_qk[:, :, :])):
                    sp.dma_start(dst, bass.AP(tensor=band_bounce.tensor,
                                              offset=band_bounce.offset + v * P * pitch + P - 1,
                                              ap=[[pitch - 1, P], [BAND, H], [1, NEAR]])).then_inc(band_read, 16)

            total_loads = n_loads[0]

            @block.tensor
            def _(pe):
                pe.wait_ge(setup_step, 3)
                for v in range(2):
                    mm = nc.tensor.matmul(single[v][0:H, 0:BAND], table[:, :], onehot[:, v, :], start=True, stop=True)
                mm.then_inc(setup_mm, 1)

            @block.vector
            def _(dve):
                nc.vector.memset(table[BUCKETS:BUCKETS + 1, :], MASKED).then_inc(setup_step, 1)
                nc.vector.memset(minus_half[:, :], -0.5).then_inc(setup_step, 1)
                dve.wait_ge(loaded, 16 * total_loads)
                nc.vector.tensor_tensor(table[0:BUCKETS, :], table[0:BUCKETS, :], table_far[:, :],
                                        ALU.subtract).then_inc(setup_step, 1)
                dve.wait_ge(setup_mm, 1)
                for v in range(2):
                    nc.vector.tensor_copy(band[:, v, :], single[v][0:H, 0:BAND]).then_inc(setup_step, 1)
                nc.vector.tensor_copy(eye_bf[:, :], eye[:, :])
                nc.vector.tensor_copy(mask_kq[:, :], mask_f[:, 0, :])
                nc.vector.tensor_copy(mask_qk[:, :], mask_f[:, 1, :])
                nc.vector.tensor_copy(expert_rows[:, :], expert_rows_f[:, :])
                dve.wait_ge(band_read, 32)
                whole = probs[:, 0:2, :, :].rearrange("p a b c -> p (a b c)").rearrange("p (h m) -> p h m", h=H)
                n = 5
                for part in range(3):
                    nc.vector.tensor_copy(bias_kq[:, part, :, :], whole).then_inc(setup_step, 1)
                    n += 1
                    if part < 2:
                        dve.wait_ge(setup_step, n)
                        nc.vector.tensor_tensor(whole, whole, bias_kq[:, part, :, :], ALU.subtract).then_inc(setup_step, 1)
                        n += 1
                        dve.wait_ge(setup_step, n)

            @block.gpsimd
            def _(pool):
                nc.gpsimd.memset(k_stack[:, :, :], 1.0)
                nc.gpsimd.memset(v_aug[:, :, :, :], 0.0).then_inc(pool_step, 1)
                pool.wait_ge(pool_step, 1)
                nc.gpsimd.memset(v_aug[:, :, :, D:D + 1], 1.0).then_inc(pool_step, 1)

        nc.all_engine_barrier(sems_to_clear=all_sems)

        with nc.Fori(0, B) as b:
            with nc.Block() as block:
                @block.sync
                def _(sp):
                    sp.dma_start(x[:, :, :], din["L0_attn_x"][bass.ds(b, 1), :, :].rearrange(
                        "a (t p) c -> p (a t) c", p=P)).then_inc(x_loaded, 16)

                    def stack_rows(parts, repeat, split, bounce, bounced, stack, rows):
                        sp.wait_ge(split, 1)
                        slot = 0
                        for n in (3, 2, 1):
                            part = 3 - n
                            for e in range(2):
                                half = slice(64 * e, 64 * e + 64)
                                src = parts[half, part:part + 1, :].broadcast_to([64, n, T]) if repeat else parts[half, 0:n, :]
                                dst = bounce[e, slot * D:(slot + n) * D, :].rearrange(
                                    "(s d) (p n) -> (d p) s n", s=n, p=PAIRS)
                                sp.dma_start(dst, src).then_inc(bounced, 16)
                            slot += n
                        sp.wait_ge(bounced, 16 * 6)
                        for e in range(2):
                            sp.dma_start(stack[64 * e:64 * e + ROWS, :, :].rearrange("r p n -> r (p n)"),
                                         bounce[e]).then_inc(rows, 16)

                    def max_rows(l, g):
                        sp.wait_ge(m_copied[l], g + 1)
                        sp.dma_start(m_bounce[l][g].rearrange("e t (p n) -> (e t p) n", p=GP),
                                     m_rows[:, g % 2, :]).then_inc(m_bounced[l][g], 16)
                        sp.wait_ge(m_bounced[l][g], 16)
                        for e in range(2):
                            r = 64 * e + ROWS
                            sp.dma_start(q_stack[r:r + MROWS, GP * g:GP * g + GP, :].rearrange("r p n -> r (p n)"),
                                         m_bounce[l][g, e]).then_inc(m_in_stack[l][g], 16)

                    for l in range(2):
                        stack_rows(k_parts, False, k_split[l], k_bounce[l], k_bounced[l], k_stack, k_rows[l])
                        stack_rows(q_parts, True, q_split[l], q_bounce[l], q_bounced[l], q_stack, q_rows[l])
                        for g in range(GROUPS):
                            max_rows(l, g)
                    sp.wait_ge(result_ready, NT)
                    sp.dma_start(out[bass.ds(b, 1), :, :].rearrange("a (t p) c -> p (a t) c", p=P),
                                 result[:, :, :]).then_inc(stored, 16)
                    sp.wait_ge(stored, 16)

                @block.tensor
                def _(pe):
                    mm = nc.tensor.matmul

                    def to_channels(n, dst_bank):
                        pe.wait_ge(normed_ready, NT * n)
                        for t in range(NT):
                            ins = nc.tensor.transpose(dst_bank[:, P * t:P * t + P], normed[n % 2][:, t, :], eye[:, :])
                        ins.then_inc(normedT_ready, 1)

                    def attention(l):
                        to_channels(l + 1, single[0][:, :])
                        pe.wait_ge(hT_ready, l + 1)
                        projections = (wk[0], wk_rot, wq[0], wq_rot) if l == 0 else (wk[1], wq[1])
                        for i, w in enumerate(projections):
                            mm(bank(i), w[:, :], hT[:, :], start=True, stop=True).then_inc(qk_proj[l], 1)
                        for t in range(NT):
                            ins = mm(bank(4)[:, P * t:P * t + P], hT[:, P * t:P * t + P], wv[l][:, :], start=True, stop=True)
                        ins.then_inc(v_proj[l], 1)

                        def free_slot(step):
                            i = RING_USES.index(step)
                            if i >= RING:
                                kind, g, n = before = RING_USES[i - RING]
                                pe.wait_ge({"M": max_done, "E": exp_done, "T": m_copied}[kind][l], nth(*before))

                        def max_piece(g, n):
                            tile, pair0, pairs = MAX_PIECES[n]
                            slot = ring[ring_slot(("M", g, n))]
                            keys = P * (tile + 1)
                            free_slot(("M", g, n))
                            for pr in range(pairs):
                                pair = GP * g + pair0 + pr
                                for e in range(2):
                                    rows = slice(64 * e, 64 * e + ROWS)
                                    ins = mm(slot[:, e, keys * pr:keys * (pr + 1)],
                                             q_stack[rows, pair, P * tile:P * tile + P], k_stack[rows, pair, 0:keys],
                                             start=True, stop=(l == 0))
                                if l == 1:
                                    for e in range(2):
                                        ins = mm(slot[:, e, keys * (pr + 1) - P:keys * (pr + 1)], eye_bf[:, :],
                                                 mask_qk[:, :], start=False, stop=True)
                            ins.then_inc(max_scores[l], 1)

                        def exp_piece(g, n):
                            tile, pair0, pairs = EXP_PIECES[n]
                            slot = ring[ring_slot(("E", g, n))]
                            queries = T - P * tile
                            near = min(NEAR, queries)
                            free_slot(("E", g, n))
                            if n == 0:
                                pe.wait_ge(m_in_stack[l][g], 32)
                            for pr in range(pairs):
                                pair = GP * g + pair0 + pr
                                for e in range(2):
                                    rows = slice(64 * e, 64 * e + ROWS + MROWS)
                                    mm(slot[:, e, queries * pr:queries * (pr + 1)],
                                       k_stack[rows, pair, P * tile:P * tile + P], q_stack[rows, pair, P * tile:T],
                                       start=True, stop=False)
                                for e in range(2):
                                    if l == 0:
                                        for part in range(3):
                                            ins = mm(slot[:, e, queries * pr:queries * pr + near], eye_bf[:, :],
                                                     bias_kq[:, part, 2 * pair + e, 0:near], start=False, stop=(part == 2))
                                    else:
                                        ins = mm(slot[:, e, queries * pr:queries * pr + P], eye_bf[:, :], mask_kq[:, :],
                                                 start=False, stop=True)
                            ins.then_inc(exp_scores[l], 1)

                        def turn_max(g):
                            slot = ring[ring_slot(("T", g, 0))]
                            free_slot(("T", g, 0))
                            pe.wait_ge(m_split[l], g + 1)
                            rows = 2 * MROWS * GP
                            view = slot[:, 0, :].bitcast(BF16)
                            for t in range(NT):
                                ins = nc.tensor.transpose(view[0:rows, P * t:P * t + P],
                                                          m_parts[:, g, t, :, :, :].rearrange("p e t q -> p (e t q)"),
                                                          eye_bf[:, :])
                            ins.then_inc(m_turned[l], 1)

                        def values(g, kt):
                            acc = single[g % 2]
                            pe.wait_ge(exp_done[l], nth("E", g, {0: 1, 1: 3, 2: 4, 3: 5}[kt]))
                            if kt == 0 and g >= 2:
                                pe.wait_ge(ctxT_copied[l], g - 1)
                            if kt == 0 and g == 0:
                                pe.wait_ge(v_ready[l], 1)
                            queries = T - P * kt
                            for j in range(GH):
                                ins = mm(acc[VCOL * j:VCOL * j + VCOL, P * kt:T], v_aug[:, kt, GH * g + j, :],
                                         probs[:, (NT * g + kt) % PBUF, j, 0:queries], start=(kt == 0), stop=(kt == NT - 1))
                            ins.then_inc(values_done[l], 1)

                        pe.wait_ge(k_rows[l], 32)
                        pe.wait_ge(q_rows[l], 32)
                        pe.wait_ge(v_ready[l], 1)
                        for kind, g, i in SCHEDULE:
                            {"M": max_piece, "E": exp_piece, "V": values}[kind](g, i) if kind != "T" else turn_max(g)

                        pe.wait_ge(ctxT_copied[l], GROUPS)
                        for t in range(NT):
                            for g in range(GROUPS):
                                ins = nc.tensor.transpose(bank(t)[:, P * g:P * g + P], ctxT[:, g, P * t:P * t + P], eye[:, :])
                            ins.then_inc(ctx_turned[l], 1)
                        for t in range(NT):
                            pe.wait_ge(ctx_ready[l], t + 1)
                            ins = nc.tensor.transpose(single[0][:, P * t:P * t + P], ctx_tok[:, t, :], eye[:, :])
                        ins.then_inc(ctx_back[l], 1)
                        pe.wait_ge(ctx_copied[l], 1)
                        for t in range(NT):
                            ins = mm(single[1][:, P * t:P * t + P], ctx_ch[:, P * t:P * t + P], wo[l][:, :], start=True, stop=True)
                        ins.then_inc(y_ready[l], 1)

                    attention(0)
                    attention(1)

                    to_channels(3, single[0][:, :])
                    pe.wait_ge(hT_ready, 3)
                    for t in range(NT):
                        ins = mm(single[1][:, EXPERTS * t:EXPERTS * t + EXPERTS], hT[:, P * t:P * t + P], gate[:, :], start=True, stop=True)
                    ins.then_inc(gate_ready, 1)

                    def up(i):
                        e, a = i // HALVES, i % HALVES
                        if i >= RING:
                            pe.wait_ge(hidden_ready, i - RING + 1)
                        mm(ring[i % RING][:, 0, :], w1[:, e, P * a:P * a + P], hT[:, :], start=True, stop=True)
                        mm(ring[i % RING][:, 1, :], w2[:, e, P * a:P * a + P], hT[:, :], start=True, stop=True).then_inc(up_ready, 1)

                    def widen(e):
                        if e:
                            pe.wait_ge(weight_bc_ready, e)
                        mm(single[1][:, :], expert_rows[:, P * e:P * e + P], weight_rows[:, :], start=True,
                           stop=True).then_inc(weight_wide, 1)

                    def down(i):
                        e, a = i // HALVES, i % HALVES
                        pe.wait_ge(hidden_w_ready, i + 1)
                        mm(single[0][:, :], w3[:, e, a, :], hidden_w[:, i % EBUF, :], start=(i == 0),
                           stop=(i == EXPERTS * HALVES - 1)).then_inc(down_done, 1)

                    up(0)
                    up(1)
                    pe.wait_ge(weight_split, 1)
                    turned = single[1][:, :].bitcast(BF16)
                    for t in range(NT):
                        ins = nc.tensor.transpose(turned[0:3 * EXPERTS, P * t:P * t + P],
                                                  weight_parts[:, t, :, :].rearrange("p s e -> p (s e)"), eye_bf[:, :])
                    ins.then_inc(weight_turned, 1)
                    pe.wait_ge(weight_copied, 1)
                    widen(0)
                    for i in range(2, EXPERTS * HALVES):
                        up(i)
                        if i % HALVES == 0:
                            widen(i // HALVES)
                        down(i - 2)
                    down(EXPERTS * HALVES - 2)
                    down(EXPERTS * HALVES - 1)
                    pe.wait_ge(moe_copied, 1)
                    for t in range(NT):
                        ins = nc.tensor.transpose(single[1][:, P * t:P * t + P], moe_ch[:, P * t:P * t + P], eye[:, :])
                    ins.then_inc(moe_turned, 1)

                @block.scalar
                def _(act):
                    def channels_in(n, scale, shift):
                        act.wait_ge(normedT_ready, n)
                        if scale is None:
                            nc.scalar.activation(hT[:, :], single[0][:, :], ACT.Identity).then_inc(hT_ready, 1)
                        else:
                            nc.scalar.activation(hT[:, :], single[0][:, :], ACT.Identity, bias=shift, scale=scale).then_inc(hT_ready, 1)

                    def attention(l):
                        if l == 1:
                            for i in range(2):
                                act.wait_ge(qk_proj[1], i + 1)
                                nc.scalar.activation(qk_f[:, i, :], bank(i), ACT.Copy).then_inc(qk_copied, 1)
                        for kind, g, i in SCHEDULE:
                            if kind == "T":
                                act.wait_ge(m_turned[l], g + 1)
                                if g >= 2:
                                    act.wait_ge(m_bounced[l][g - 2], 16)
                                rows = 2 * MROWS * GP
                                view = ring[ring_slot(("T", g, 0))][:, 0, :].bitcast(BF16)
                                nc.scalar.activation(m_rows[:, g % 2, :], view[0:rows, 0:T], ACT.Copy).then_inc(m_copied[l], 1)
                            elif kind == "E":
                                tile, pair0, pairs = EXP_PIECES[i]
                                slot = ring[ring_slot((kind, g, i))]
                                queries = T - P * tile
                                buf = probs[:, (NT * g + tile) % PBUF, :, :]
                                act.wait_ge(exp_scores[l], nth("E", g, i))
                                if pair0 == 0 and NT * g + tile >= PBUF:
                                    before = NT * g + tile - PBUF
                                    act.wait_ge(values_done[l], nth("V", before // NT, before % NT))
                                src = slot[:, :, 0:queries * pairs].rearrange("p e (r q) -> p e r q", r=pairs)
                                dst = buf[:, 2 * pair0:2 * pair0 + 2 * pairs, 0:queries].rearrange("p (r e) q -> p e r q", e=2)
                                if pairs == 1:
                                    src, dst = src[:, :, 0, :], dst[:, :, 0, :]
                                nc.scalar.activation(dst, src, ACT.Exp, scale=SCALE).then_inc(exp_done[l], 1)
                            elif kind == "V" and i == NT - 1:
                                act.wait_ge(values_done[l], nth("V", g, i))
                                nc.scalar.activation(ctxT[:, g, :], single[g % 2][:, :], ACT.Copy).then_inc(ctxT_copied[l], 1)
                        act.wait_ge(ctx_back[l], 1)
                        nc.scalar.activation(ctx_ch[:, :], single[0][:, :], ACT.Copy).then_inc(ctx_copied[l], 1)

                    channels_in(1, None, None)
                    attention(0)
                    channels_in(2, ln_cols[:, 0:1], ln_cols[:, 1:2])
                    attention(1)
                    channels_in(3, ln_cols[:, 2:3], ln_cols[:, 3:4])

                    def tanh_of(i):
                        act.wait_ge(up_ready, i + 1)
                        if i >= EBUF:
                            act.wait_ge(gated_ready, i - EBUF + 1)
                        nc.scalar.activation(tanh_t[:, i % EBUF, :], ring[i % RING][:, 0, :], ACT.Tanh, scale=0.5).then_inc(tanh_ready, 1)

                    def wide_weight(e):
                        act.wait_ge(weight_wide, e + 1)
                        if e >= 2:
                            act.wait_ge(hidden_w_ready, HALVES * (e - 1))
                        nc.scalar.activation(weight_bc[:, e % 2, :], single[1][:, :], ACT.Copy, scale=0.5).then_inc(weight_bc_ready, 1)

                    act.wait_ge(gap_ready, 1)
                    nc.scalar.activation(gap_exp[:, :], gap[:, :], ACT.Exp).then_inc(gap_exp_ready, 1)
                    tanh_of(0)
                    tanh_of(1)
                    act.wait_ge(weight_turned, 1)
                    nc.scalar.activation(weight_rows[:, :], single[1][:, :].bitcast(BF16)[0:3 * EXPERTS, 0:T], ACT.Copy).then_inc(weight_copied, 1)
                    wide_weight(0)
                    for i in range(2, EXPERTS * HALVES):
                        tanh_of(i)
                        if i % HALVES == 0:
                            wide_weight(i // HALVES)
                    act.wait_ge(down_done, EXPERTS * HALVES)
                    nc.scalar.activation(moe_ch[:, :], single[0][:, :], ACT.Copy).then_inc(moe_copied, 1)

                def split3(engine, queue, whole, rest, parts, step, last):
                    step(engine.tensor_copy(parts[0], whole))
                    step(engine.tensor_tensor(rest, whole, parts[0], ALU.subtract))
                    step(engine.tensor_copy(parts[1], rest))
                    engine.tensor_tensor(parts[2], rest, parts[1], ALU.subtract).then_inc(last, 1)

                @block.gpsimd
                def _(pool):
                    steps = [0]

                    def step(ins):
                        steps[0] += 1
                        ins.then_inc(pool_step, 1)
                        pool.wait_ge(pool_step, steps[0])

                    def inverse_root(n):
                        pool.wait_ge(var_ready, n + 1)
                        nc.gpsimd.tensor_tensor(rstd[:, n, :], var_eps[:, n, :], minus_half[:, :], ALU.pow).then_inc(rstd_ready, 1)

                    def attention(l):
                        if l == 0:
                            pool.wait_ge(rope_ready, 2)
                            step(nc.gpsimd.tensor_tensor(qk_f[:, 1, :], rope_a[:, 1, :], rope_b[:, 1, :], ALU.add))
                        else:
                            pool.wait_ge(qk_copied, 2)
                        split3(nc.gpsimd, pool, qk_f[:, 1, :], qk_rest[:, 1, :], [q_parts[:, i, :] for i in range(3)], step, q_split[l])
                        for g in range(GROUPS):
                            pool.wait_ge(group_max[l], g + 1)
                            shape = lambda i: m_parts[:, g, :, :, i, :].rearrange("p t e r -> p t r e")
                            view = lambda m: m[:, g, :, :].rearrange("p t (r e) -> p t r e", e=2)
                            parts = [shape(i) for i in range(3)]
                            step(nc.gpsimd.tensor_copy(parts[0], view(neg_max)))
                            step(nc.gpsimd.tensor_tensor(view(m_rest), view(neg_max), parts[0], ALU.subtract))
                            step(nc.gpsimd.tensor_copy(parts[1], view(m_rest)))
                            nc.gpsimd.tensor_tensor(parts[2], view(m_rest), parts[1], ALU.subtract).then_inc(m_split[l], 1)

                    inverse_root(0)
                    attention(0)
                    inverse_root(1)
                    inverse_root(2)
                    inverse_root(3)
                    attention(1)
                    inverse_root(4)
                    for i in range(EXPERTS * HALVES):
                        pool.wait_ge(hidden_ready, i + 1)
                        pool.wait_ge(weight_bc_ready, i // HALVES + 1)
                        if i >= EBUF:
                            pool.wait_ge(down_done, i - EBUF + 1)
                        nc.gpsimd.tensor_tensor(hidden_w[:, i % EBUF, :], hidden[:, i % EBUF, :], weight_bc[:, (i // HALVES) % 2, :],
                                                ALU.mult).then_inc(hidden_w_ready, 1)
                    inverse_root(5)

                @block.vector
                def _(dve):
                    steps, nears = [0], [0]

                    def step(ins):
                        steps[0] += 1
                        ins.then_inc(vector_step, 1)
                        dve.wait_ge(vector_step, steps[0])

                    def statistics(src, n):
                        for t in range(NT):
                            ins = nc.vector.bn_stats(stats[:, t, :], src[:, t, :])
                        step(ins)
                        for t in range(NT):
                            ins = nc.vector.bn_aggr(mean_var[:, n, t, :], stats[:, t, :])
                        step(ins)
                        nc.vector.tensor_scalar(var_eps[:, n, :], mean_var[:, n, :, 1], EPS, None, ALU.add).then_inc(var_ready, 1)
                        dve.wait_ge(rstd_ready, n + 1)

                    def normalise(dst, src, n, done=None):
                        for t in range(NT):
                            ins = nc.vector.tensor_scalar(dst[:, t, :], src[:, t, :], mean_var[:, n, t, 0:1], rstd[:, n, t:t + 1],
                                                          ALU.subtract, ALU.mult)
                            if done is not None:
                                ins.then_inc(done, 1)
                        if done is None:
                            step(ins)

                    def rotate(i, first):
                        col = 2 - 2 * i
                        dve.wait_ge(qk_proj[0], first + 1)
                        nc.vector.scalar_tensor_tensor(rope_a[:, i, :], bank(first), bias_cols[:, col:col + 1], cos_t[:, :],
                                                       ALU.add, ALU.mult)
                        dve.wait_ge(qk_proj[0], first + 2)
                        return nc.vector.scalar_tensor_tensor(rope_b[:, i, :], bank(first + 1), bias_cols[:, col + 1:col + 2],
                                                              sin_t[:, :], ALU.add, ALU.mult)

                    def attention(l):
                        if l == 0:
                            step(rotate(0, 0))
                            rotate(1, 2).then_inc(rope_ready, 2)
                            step(nc.vector.tensor_tensor(qk_f[:, 0, :], rope_a[:, 0, :], rope_b[:, 0, :], ALU.add))
                        else:
                            dve.wait_ge(qk_copied, 1)
                        split3(nc.vector, dve, qk_f[:, 0, :], qk_rest[:, 0, :], [k_parts[:, i, :] for i in range(3)], step, k_split[l])
                        dve.wait_ge(v_proj[l], 1)
                        v_src = bank(4).rearrange("p (t h d) -> p t h d", t=NT, h=H)
                        for t in range(NT):
                            if l == 0:
                                ins = nc.vector.tensor_tensor(v_aug[:, t, :, 0:D], v_src[:, t, :, :],
                                                              bv_row[:, :].rearrange("p (h d) -> p h d", h=H), ALU.add)
                            else:
                                ins = nc.vector.tensor_copy(v_aug[:, t, :, 0:D], v_src[:, t, :, :])
                        ins.then_inc(v_ready[l], 1)
                        for kind, g, n in SCHEDULE:
                            if kind != "M":
                                continue
                            tile, pair0, pairs = MAX_PIECES[n]
                            slot = ring[ring_slot((kind, g, n))]
                            keys = P * (tile + 1)
                            heads = 2 * pairs
                            h0 = GH * g + 2 * pair0
                            dve.wait_ge(max_scores[l], nth("M", g, n))
                            scores = slot[:, :, 0:keys * pairs].rearrange("p e (r k) -> p e r k", r=pairs)
                            if pairs == 1:
                                scores = scores[:, :, 0, :]
                            if l == 1:
                                dst = neg_max[:, g, tile, 2 * pair0:2 * pair0 + heads].rearrange("p (r e) -> p e r", e=2)
                                if pairs == 1:
                                    dst = dst[:, :, 0]
                                nc.vector.tensor_reduce(dst, scores, AX_X, ALU.max, negate=True).then_inc(max_done[l], 1)
                                if n == len(MAX_PIECES) - 1:
                                    dve.wait_ge(max_done[l], nth("M", g, n))
                                    nc.vector.engine_nop().then_inc(group_max[l], 1)
                                continue
                            if tile >= 2:
                                far = far_max[:, tile, h0:h0 + heads]
                                nc.vector.tensor_reduce(far, scores[:, :, 0:keys - NEAR], AX_X, ALU.max)
                            near = min(NEAR, keys)
                            for r in range(pairs):
                                for e in range(2):
                                    h = h0 + 2 * r + e
                                    if nears[0] >= NBUF:
                                        dve.wait_ge(near_added, nears[0] - NBUF + 1)
                                    ins = nc.vector.tensor_tensor_reduce(
                                        out=near_sum[:, nears[0] % NBUF, 0:near], in0=slot[:, e, keys * (r + 1) - near:keys * (r + 1)],
                                        in1=bias_qk[:, h, NEAR - near:NEAR], scale=1.0, scalar=2.0 * MASKED, op0=ALU.add, op1=ALU.max,
                                        accum_out=near_max[:, tile, h:h + 1]).then_inc(near_added, 1)
                                    nears[0] += 1
                            dve.wait_ge(near_added, nears[0])
                            nc.vector.engine_nop().then_inc(max_done[l], 1)
                            if n == len(MAX_PIECES) - 1:
                                hs = slice(GH * g, GH * g + GH)
                                nc.vector.tensor_scalar(neg_max[:, g, 0:2, :], near_max[:, 0:2, hs], -1.0, None, ALU.mult)
                                step(nc.vector.tensor_tensor(m_rest2[:, g, 2:NT, :], near_max[:, 2:NT, hs], far_max[:, 2:NT, hs], ALU.max))
                                nc.vector.tensor_scalar(neg_max[:, g, 2:NT, :], m_rest2[:, g, 2:NT, :], -1.0, None,
                                                        ALU.mult).then_inc(group_max[l], 1)
                        for t in range(NT):
                            dve.wait_ge(ctx_turned[l], t + 1)
                            src = bank(t).rearrange("p (h v) -> p h v", h=H)
                            step(nc.vector.reciprocal(row_inv[:, t, :], src[:, :, D]))
                            nc.vector.tensor_tensor(ctx_tok[:, t, :].rearrange("p (h d) -> p h d", h=H), src[:, :, 0:D],
                                                    row_inv[:, t, :].unsqueeze(2).broadcast_to([P, H, D]),
                                                    ALU.mult).then_inc(ctx_ready[l], 1)
                        dve.wait_ge(y_ready[l], 1)

                    def plus_row(dst, psum, row):
                        step(nc.vector.tensor_tensor(dst[:, :, :], psum.rearrange("p (t c) -> p t c", t=NT),
                                                     row[:, :].unsqueeze(1).broadcast_to([P, NT, C]), ALU.add))

                    x1, u, u2, branch = resid
                    dve.wait_ge(x_loaded, 16)
                    statistics(x, 0)
                    normalise(normed[1], x, 0, normed_ready)
                    attention(0)
                    plus_row(branch, single[1][:, :], bo_row[0])
                    statistics(branch, 1)
                    normalise(x1, branch, 1)
                    step(nc.vector.tensor_tensor(x1[:, :, :], x1[:, :, :], x[:, :, :], ALU.add))
                    statistics(x1, 2)
                    normalise(u, x1, 2)
                    statistics(u, 3)
                    normalise(normed[0], u, 3, normed_ready)
                    attention(1)
                    plus_row(u2, single[1][:, :], bo_row[1])
                    step(nc.vector.tensor_tensor(u2[:, :, :], u2[:, :, :], u[:, :, :], ALU.add))
                    statistics(u2, 4)
                    normalise(normed[1], u2, 4, normed_ready)

                    dve.wait_ge(gate_ready, 1)
                    step(nc.vector.tensor_copy(gate_s[:, :, :], single[1][:, 0:NT * EXPERTS].rearrange("p (t e) -> p t e", t=NT)))
                    for t in range(NT):
                        ins = nc.vector.max(top8[:, t, :], gate_s[:, t, :])
                    step(ins)
                    nc.vector.tensor_tensor(gap[:, :], top8[:, :, 1], top8[:, :, 0], ALU.subtract).then_inc(gap_ready, 1)
                    for t in range(NT):
                        ins = nc.vector.max_index(top_ids[:, t, :], top8[:, t, :], gate_s[:, t, :])
                    step(ins)
                    step(nc.vector.tensor_copy(top_ids_f[:, :, :], top_ids[:, :, 0:2]))
                    dve.wait_ge(gap_exp_ready, 1)
                    step(nc.vector.tensor_scalar(gap_den[:, :], gap_exp[:, :], 1.0, None, ALU.add))
                    step(nc.vector.reciprocal(top_p[:, 0, :], gap_den[:, :]))
                    step(nc.vector.tensor_tensor(top_p[:, 1, :], top_p[:, 0, :], gap_exp[:, :], ALU.mult))
                    for k in range(2):
                        step(nc.vector.tensor_tensor(pick[:, k, :, :], expert_ids[:, :, :],
                                                     top_ids_f[:, :, k].unsqueeze(2).broadcast_to([P, NT, EXPERTS]), ALU.is_equal))
                        step(nc.vector.tensor_tensor(pick_w[:, k, :, :], pick[:, k, :, :],
                                                     top_p[:, k, :].unsqueeze(2).broadcast_to([P, NT, EXPERTS]), ALU.mult))
                    step(nc.vector.tensor_tensor(weight[:, :, :], pick_w[:, 0, :, :], pick_w[:, 1, :, :], ALU.add))
                    split3(nc.vector, dve, weight[:, :, :], weight_rest[:, 0, :, :],
                           [weight_parts[:, :, i, :] for i in range(3)], step, weight_split)

                    for i in range(EXPERTS * HALVES):
                        dve.wait_ge(tanh_ready, i + 1)
                        nc.vector.scalar_tensor_tensor(gated[:, i % EBUF, :], tanh_t[:, i % EBUF, :], 1.0, ring[i % RING][:, 0, :],
                                                       ALU.add, ALU.mult).then_inc(gated_ready, 1)
                        dve.wait_ge(gated_ready, i + 1)
                        if i >= EBUF:
                            dve.wait_ge(hidden_w_ready, i - EBUF + 1)
                        nc.vector.tensor_tensor(hidden[:, i % EBUF, :], gated[:, i % EBUF, :], ring[i % RING][:, 1, :],
                                                ALU.mult).then_inc(hidden_ready, 1)

                    dve.wait_ge(moe_turned, 1)
                    step(nc.vector.tensor_tensor(branch[:, :, :], u2[:, :, :], single[1][:, :].rearrange("p (t c) -> p t c", t=NT), ALU.add))
                    statistics(branch, 5)
                    normalise(u, branch, 5)
                    for t in range(NT):
                        nc.vector.tensor_tensor(result[:, t, :], u[:, t, :], x1[:, t, :], ALU.add).then_inc(result_ready, 1)

            nc.all_engine_barrier(sems_to_clear=all_sems)


AS_GIVEN = ["L0_attn_x", "L0_attn_Wv", "L0_attn_bv", "L0_attn_Wp", "L0_attn_bp", "L0_attn_rel_bias_table",
            "L0_ffn_ln1_scale", "L0_ffn_ln1_shift", "L0_ffn_wv", "L0_ffn_wo", "L0_ffn_bo", "L0_ffn_ln2_scale",
            "L0_ffn_ln2_shift", "L0_ffn_gate_w", "L0_ffn_w1", "L0_ffn_w2", "L0_ffn_w3"]


def by_parity(w, partner=False):
    w = np.asarray(w)
    w = w.reshape(w.shape[:-1] + (PAIRS, 2, D))
    if partner:
        w = np.concatenate([w[..., D // 2:], w[..., :D // 2]], axis=-1)
    return np.moveaxis(w, -3, -1).reshape(w.shape[:-3] + (C,))


def kernel(**inputs):
    import concourse.bacc as bacc
    from concourse.bass_utils import run_bass_kernel_spmd

    laid_out = {name: inputs[name] for name in AS_GIVEN}
    laid_out["qk_weights"] = np.stack([
        by_parity(inputs["L0_attn_Wq"]), by_parity(inputs["L0_attn_Wk"]),
        by_parity(inputs["L0_ffn_wq"]), by_parity(inputs["L0_ffn_wk"]),
        by_parity(inputs["L0_attn_Wq"], True), by_parity(inputs["L0_attn_Wk"], True)])
    laid_out["qk_biases"] = np.stack([
        by_parity(inputs["L0_attn_bq"]), by_parity(inputs["L0_attn_bq"], True),
        by_parity(inputs["L0_attn_bk"]), by_parity(inputs["L0_attn_bk"], True)], axis=1)
    nc = bacc.Bacc("TRN2", target_bir_lowering=False, num_devices=1)
    arrays, din, const = {}, {}, {}
    for name, a in laid_out.items():
        a = np.ascontiguousarray(a)
        arrays[f"in_{name}"] = a
        din[name] = nc.dram_tensor(f"in_{name}", a.shape, mybir.dt.from_np(a.dtype), kind="ExternalInput").ap()
    for name, a in shape_constants().items():
        arrays[f"const_{name}"] = a
        const[name] = nc.dram_tensor(f"const_{name}", a.shape, F32, kind="ExternalInput").ap()
    out = nc.dram_tensor("out", (B, T, C), F32, kind="ExternalOutput").ap()
    sandwich(nc, din, const, out)
    r = run_bass_kernel_spmd(nc, [arrays], core_ids=[0])
    return r.results[0]["out"]
```

```python
from contextlib import ExitStack

import numpy as np

import concourse.bass as bass
from concourse import mybir

F32 = mybir.dt.float32
BF16 = mybir.dt.bfloat16
U32 = mybir.dt.uint32
ALU = mybir.AluOpType
ACT = mybir.ActivationFunctionType
AX_X = mybir.AxisListType.X

B, T, C = 16, 512, 128
H = 16
D = C // H
P = 128
NT = T // P
PAIRS = H // 2
GROUPS = 4
GH = H // GROUPS
GP = GH // 2
SCALE = float(1.0 / np.sqrt(D))
EPS = 1e-5
SLOTS = 6
ROWS = SLOTS * D
MROWS = 3
BUCKETS = 32
BAND = 384
NEAR = 2 * P
MASKED = -1e30
EXPERTS, HID = 8, 256
HALVES = HID // P
VCOL = 32
NORMS = 6
RING = 3
PBUF = 3
EBUF = 3
NBUF = 2

UNITS = EXPERTS * HALVES

MAX_PIECES = [(0, 0, 2), (1, 0, 2), (2, 0, 1), (2, 1, 1), (3, 0, 1), (3, 1, 1)]
VALUES_AFTER = {2: 0, 4: 1, 5: 2}
EXP_PIECES = [(0, 0, 1), (0, 1, 1), (1, 0, 1), (1, 1, 1), (2, 0, 2), (3, 0, 2)]


def attention_steps(l):
    order = [("max", l, 0, i) for i in range(6)]
    order += [("max", l, 1, i) for i in range(3)] + [("turn_max", l, 0)] + [("max", l, 1, i) for i in range(3, 6)]
    for g in range(GROUPS):
        for i in range(len(EXP_PIECES)):
            if g + 2 < GROUPS:
                order.append(("max", l, g + 2, i))
            order.append(("exp", l, g, i))
            if i in VALUES_AFTER:
                order.append(("values", l, g, VALUES_AFTER[i]))
            if i == 0 and g:
                order.append(("values", l, g - 1, NT - 1))
            if i == 1 and g + 1 < GROUPS:
                order.append(("turn_max", l, g + 1))
    order.append(("values", l, GROUPS - 1, NT - 1))
    return order


def expert_steps():
    order = [("up", 0), ("up", 1), ("widen", 0)]
    for i in range(2, UNITS):
        order.append(("up", i))
        if i % HALVES == 0:
            order.append(("widen", i // HALVES))
        order.append(("down", i - 2))
    return order + [("down", UNITS - 2), ("down", UNITS - 1)]


def projection_steps(l):
    return [("to_channels", l), ("project_k", l), ("project_q", l), ("project_v", l), ("split", l)]


def output_steps(l):
    return [("context", l, 0), ("context", l, 1), ("context_back", l), ("attended", l)]


def spread(core, between, first, last):
    out, at = [], [int(len(core) * (first + (last - first) * k / len(between))) for k in range(len(between))]
    for k, step in enumerate(core):
        out += [between[m] for m in range(len(between)) if at[m] == k]
        out.append(step)
    return out


def body_steps(older, newer):
    if not older:
        return ([("stats", 0), ("norm", 0)] + projection_steps(0) + attention_steps(0) + output_steps(0)
                + [("stats", 1), ("norm", 1), ("stats", 2), ("norm", 2), ("stats", 3), ("norm", 3)] + projection_steps(1))
    first, second = [], []
    if newer:
        first = [("stats", 0), ("norm", 0)] + projection_steps(0)
        second = (output_steps(0) + [("stats", 1), ("norm", 1), ("stats", 2), ("norm", 2), ("stats", 3), ("norm", 3)]
                  + projection_steps(1))
    mixture = output_steps(1) + [("stats", 4), ("norm", 4), ("to_channels", 2), ("gate",), ("turn_weights",)]
    steps = spread(attention_steps(1), first, 0.1, 0.6) if newer else attention_steps(1)
    steps += spread(attention_steps(0), mixture, 0.02, 0.8) if newer else mixture
    steps += spread(expert_steps(), second, 0.03, 0.75) if newer else expert_steps()
    return steps + [("finish",), ("stats", 5), ("norm", 5)]


RING_KINDS = ("max", "turn_max", "exp", "context", "context_back", "attended", "to_channels", "project_k", "project_q",
              "project_v", "gate", "turn_weights", "up", "widen", "finish")


def nth(kind, l, g, i):
    return [s for s in attention_steps(l) if s[0] == kind].index((kind, l, g, i)) + 1


def heads_by(g, i):
    return sum(2 * MAX_PIECES[s[3]][2] for s in [s for s in attention_steps(0) if s[0] == "max"][:nth("max", 0, g, i)])


def shape_constants():
    inv = 1.0 / 10000.0 ** (np.arange(0, D, 2, dtype=np.float32) / D)
    freqs = np.arange(T, dtype=np.float32)[:, None] * inv[None, :].astype(np.float32)
    freqs = np.concatenate([freqs, freqs], axis=-1)
    cos, sin = np.cos(freqs).T, np.sin(freqs).T
    sign = np.where(np.arange(D) < D // 2, -1.0, 1.0)[:, None]
    spread = lambda x: np.broadcast_to(x[None, :, None, :], (2, D, PAIRS, T)).reshape(P, T)
    n = np.arange(BAND) - (P - 1)
    exact = BUCKETS // 2
    far = exact + (np.log(np.maximum(n, 1).astype(np.float32) / exact) / np.log(128 / exact)
                   * (BUCKETS - exact)).astype(np.int32)
    bucket = np.where(n < exact, n, np.minimum(far, BUCKETS - 1))
    bucket = np.where(n < 0, BUCKETS, bucket)
    forward = (np.arange(BUCKETS + 1)[:, None] == bucket[None, :])
    mirrored_n = (NEAR - 1) - np.arange(BAND)
    backward = np.zeros((BUCKETS + 1, BAND), bool)
    for m in range(BAND - 1):
        backward[:, m] = forward[:, mirrored_n[m] + P - 1]
    eye = np.eye(P)
    causal = np.where(np.arange(P)[:, None] > np.arange(P)[None, :], MASKED, 0.0)
    experts = np.zeros((3, EXPERTS, EXPERTS, P))
    for e in range(EXPERTS):
        experts[:, e, e, :] = 1.0
    f = lambda x: np.ascontiguousarray(x, dtype=np.float32)
    return {
        "cos": f(spread(cos)), "sin": f(spread(sin * sign)),
        "band": f(np.stack([forward, backward], axis=1)),
        "eye": f(eye),
        "mask_kq": f(causal), "mask_qk": f(causal.T),
        "expert_rows": f(experts.reshape(3 * EXPERTS, EXPERTS * P)),
        "expert_ids": f(np.broadcast_to(np.arange(EXPERTS), (P, NT, EXPERTS))),
    }


def sandwich(nc, din, const, out):
    ctx = ExitStack()
    with ctx:
        def sb(name, shape, dt=F32):
            return ctx.enter_context(nc.sbuf_tensor(name, shape, dt))

        sems = []

        def sem(name):
            s = ctx.enter_context(nc.semaphore(name))
            sems.append(s)
            return s

        def sem2(name):
            return [sem(f"{name}{i}") for i in range(2)]

        def scratch(name, shape, dt):
            return nc.dram_tensor(name, shape, dt, kind="Internal").ap()

        q_bounce = [scratch(f"q_bounce{i}", [2, ROWS, PAIRS * T], BF16) for i in range(2)]
        k_bounce = [scratch(f"k_bounce{i}", [2, ROWS, PAIRS * T], BF16) for i in range(2)]
        m_bounce = [scratch(f"m_bounce{i}", [GROUPS, 2, MROWS, GP * T], BF16) for i in range(2)]
        band_bounce = scratch("band_bounce", [2, P, H, BAND], F32)

        cos_t, sin_t = sb("cos_t", [P, T]), sb("sin_t", [P, T])
        eye = sb("eye", [P, P])
        eye_bf = sb("eye_bf", [P, P], BF16)
        mask_kq, mask_qk = sb("mask_kq", [P, P], BF16), sb("mask_qk", [P, P], BF16)
        table = sb("table", [BUCKETS + 1, H])
        table_far = sb("table_far", [BUCKETS, H])
        bias_qk = sb("bias_qk", [P, H, NEAR])
        bias_kq = sb("bias_kq", [P, 3, H, NEAR], BF16)
        expert_rows = sb("expert_rows", [3 * EXPERTS, EXPERTS * P], BF16)
        expert_ids = sb("expert_ids", [P, NT, EXPERTS])
        wq = [sb(f"wq{i}", [P, C]) for i in range(2)]
        wk = [sb(f"wk{i}", [P, C]) for i in range(2)]
        wv = [sb(f"wv{i}", [P, C]) for i in range(2)]
        wo = [sb(f"wo{i}", [P, C]) for i in range(2)]
        wq_rot, wk_rot = sb("wq_rot", [P, C]), sb("wk_rot", [P, C])
        bias_cols = sb("bias_cols", [P, 4])
        ln_cols = sb("ln_cols", [P, 4])
        bv_row, bo_row = sb("bv_row", [P, C]), [sb(f"bo_row{i}", [P, C]) for i in range(2)]
        gate = sb("gate", [P, EXPERTS])
        w1, w2 = sb("w1", [P, EXPERTS, HID]), sb("w2", [P, EXPERTS, HID])
        w3 = sb("w3", [P, EXPERTS, HALVES, C])
        minus_half = sb("minus_half", [P, NT])

        x = sb("x", [P, NT, C])
        x1, x1_older, u, u2, branch = (sb(n, [P, NT, C]) for n in ("x1", "x1_older", "u", "u2", "branch"))
        normed = [sb(f"normed{i}", [P, NT, C]) for i in range(2)]
        stats_t = sb("stats_t", [P, NT, 6])
        mean_var = sb("mean_var", [P, NORMS, NT, 2])
        var_eps = sb("var_eps", [P, NORMS, NT])
        rstd = sb("rstd", [P, NORMS, NT])
        hT = [sb(f"hT{i}", [P, T]) for i in range(2)]
        rope_a, rope_b = sb("rope_a", [P, 2, T]), sb("rope_b", [P, 2, T])
        qk_f = sb("qk_f", [P, 2, T])
        qk_rest = rope_a
        q_parts, k_parts = sb("q_parts", [P, 3, T], BF16), sb("k_parts", [P, 3, T], BF16)
        q_stack = [sb(f"q_stack{i}", [P, PAIRS, T], BF16) for i in range(2)]
        k_stack = [sb(f"k_stack{i}", [P, PAIRS, T], BF16) for i in range(2)]
        v_aug = [sb(f"v_aug{i}", [P, NT, H, VCOL]) for i in range(2)]
        near_sum = sb("near_sum", [P, NBUF, NEAR])
        near_max, far_max = sb("near_max", [P, NT, H]), sb("far_max", [P, NT, H])
        neg_max = sb("neg_max", [P, GROUPS, NT, GH])
        m_rest = sb("m_rest", [P, GROUPS, NT, GH])
        m_most = sb("m_most", [P, GROUPS, NT, GH])
        m_parts = sb("m_parts", [P, GROUPS, NT, 2, MROWS, GP], BF16)
        m_rows = sb("m_rows", [2 * MROWS * GP, 2, T], BF16)
        probs = sb("probs", [P, PBUF, GH, T])
        ctxT = sb("ctxT", [P, GROUPS, T])
        flat = probs[:, :, :, :].rearrange("p a b n -> p (a b n)")
        bias_whole = flat[:, 0:H * NEAR].rearrange("p (h m) -> p h m", h=H)
        onehot = flat[0:BUCKETS + 1, H * NEAR:H * NEAR + 2 * BAND].rearrange("p (v m) -> p v m", v=2)
        band = flat[0:H, H * NEAR + 2 * BAND:H * NEAR + 4 * BAND].rearrange("p (v m) -> p v m", v=2)
        expert_rows_f = ctxT[0:3 * EXPERTS, :, :].rearrange("p g n -> p (g n)")[:, 0:EXPERTS * P]
        mask_f = ctxT[:, GROUPS - 1, 0:2 * P].rearrange("p (v n) -> p v n", v=2)
        row_inv = sb("row_inv", [P, NT, H])
        ctx_tok = sb("ctx_tok", [P, NT, C])
        ctx_ch = rope_a[:, 0, :]
        gate_s = sb("gate_s", [P, NT, EXPERTS])
        top8 = sb("top8", [P, NT, EXPERTS])
        top_ids = sb("top_ids", [P, NT, EXPERTS], U32)
        top_ids_f = sb("top_ids_f", [P, NT, 2])
        gap = sb("gap", [P, NT])
        gap_exp = sb("gap_exp", [P, NT])
        gap_den = sb("gap_den", [P, NT])
        top_p = sb("top_p", [P, 2, NT])
        pick = sb("pick", [P, 2, NT, EXPERTS])
        pick_w = sb("pick_w", [P, 2, NT, EXPERTS])
        weight = sb("weight", [P, NT, EXPERTS])
        weight_rest = sb("weight_rest", [P, 2, NT, EXPERTS])
        weight_parts = sb("weight_parts", [P, NT, 3, EXPERTS], BF16)
        weight_rows = sb("weight_rows", [3 * EXPERTS, T], BF16)
        weight_bc = rope_b
        spare = probs[:, :, :, :].rearrange("p a b n -> p (a b) n")
        tanh_t, gated, hidden, hidden_w = (spare[:, EBUF * i:EBUF * (i + 1), :] for i in range(4))
        moe_ch = tanh_t[:, 0, :]
        result = tanh_t[:, 1, :].rearrange("p (t c) -> p t c", t=NT)

        ring = [ctx.enter_context(nc.psum_tensor(f"ring{i}", [P, 2, T], F32)) for i in range(RING)]
        single = [ctx.enter_context(nc.psum_tensor(f"single{i}", [P, T], F32)) for i in range(2)]

        loaded, setup_step, setup_mm = sem("loaded"), sem("setup_step"), sem("setup_mm")
        band_written, band_read = sem("band_written"), sem("band_read")
        x_loaded = sem("x_loaded")
        vector_step, pool_step = sem("vector_step"), sem("pool_step")
        var_ready, rstd_ready = ([sem(f"{n}{i}") for i in range(NORMS)] for n in ("var_ready", "rstd_ready"))
        normed_ready, normed_turned, hT_ready = ([sem(f"{n}{i}") for i in range(3)] for n in ("normed_ready", "normed_turned", "hT_ready"))
        k_proj, q_proj, v_proj = sem2("k_proj"), sem2("q_proj"), sem2("v_proj")
        k_read, q_read = sem2("k_read"), sem2("q_read")
        q_split, k_split, v_ready = sem2("q_split"), sem2("k_split"), sem2("v_ready")
        q_bounced, k_bounced, q_rows, k_rows = (sem2(n) for n in ("q_bounced", "k_bounced", "q_rows", "k_rows"))
        max_scores, heads_maxed = sem2("max_scores"), sem2("heads_maxed")
        group_max, m_split = sem2("group_max"), sem2("m_split")
        m_turned, m_copied = sem2("m_turned"), sem2("m_copied")
        m_bounced = [[sem(f"m_bounced{i}_{g}") for g in range(GROUPS)] for i in range(2)]
        m_in_stack = [[sem(f"m_in_stack{i}_{g}") for g in range(GROUPS)] for i in range(2)]
        exp_scores, exp_done = sem2("exp_scores"), sem2("exp_done")
        values_done, ctxT_copied = sem2("values_done"), sem2("ctxT_copied")
        ctx_turned, ctx_ready = sem2("ctx_turned"), sem2("ctx_ready")
        ctx_back, ctx_copied, y_ready, y_read = sem2("ctx_back"), sem2("ctx_copied"), sem2("y_ready"), sem2("y_read")
        x1_kept = sem("x1_kept")
        gate_ready, gate_read, gap_ready, gap_exp_ready = sem("gate_ready"), sem("gate_read"), sem("gap_ready"), sem("gap_exp_ready")
        weight_split, weight_turned, weight_copied = sem("weight_split"), sem("weight_turned"), sem("weight_copied")
        weight_wide, weight_bc_ready = sem("weight_wide"), sem("weight_bc_ready")
        up_ready, tanh_ready, gated_ready = sem("up_ready"), sem("tanh_ready"), sem("gated_ready")
        hidden_ready, hidden_w_ready = sem("hidden_ready"), sem("hidden_w_ready")
        down_done, moe_copied, moe_turned, moe_read = sem("down_done"), sem("moe_copied"), sem("moe_turned"), sem("moe_read")
        result_ready, stored = sem("result_ready"), sem("stored")
        all_sems = range(min(s.num for s in sems), max(s.num for s in sems) + 1)

        n_loads = [0]
        with nc.Block() as block:
            def load(eng, dst, src):
                n_loads[0] += 1
                eng.dma_start(dst, src).then_inc(loaded, 16)

            def across(name):
                v = din[name]
                return bass.AP(tensor=v.tensor, offset=v.offset, ap=[[0, P], [1, C]])

            @block.sync
            def _(sp):
                load(sp, onehot[:, :, :], const["band"])
                load(sp, table[0:BUCKETS, :], din["L0_attn_rel_bias_table"])
                tb = din["L0_attn_rel_bias_table"]
                load(sp, table_far[:, :], bass.AP(tensor=tb.tensor, offset=tb.offset + (BUCKETS - 1) * H,
                                                  ap=[[0, BUCKETS], [1, H]]))
                load(sp, cos_t[:, :], const["cos"])
                load(sp, sin_t[:, :], const["sin"])
                load(sp, eye[:, :], const["eye"])
                load(sp, mask_f[:, 0, :], const["mask_kq"])
                load(sp, mask_f[:, 1, :], const["mask_qk"])
                load(sp, expert_rows_f[:, :], const["expert_rows"])
                load(sp, expert_ids[:, :, :], const["expert_ids"])
                for i, w in enumerate((wq[0], wk[0], wq[1], wk[1], wq_rot, wk_rot)):
                    load(sp, w[:, :], din["qk_weights"][i])
                load(sp, bias_cols[:, :], din["qk_biases"])
                load(sp, wv[0][:, :], din["L0_attn_Wv"])
                load(sp, wv[1][:, :], din["L0_ffn_wv"])
                load(sp, wo[0][:, :], din["L0_attn_Wp"])
                load(sp, wo[1][:, :], din["L0_ffn_wo"])
                for i, n in enumerate(("ln1_scale", "ln1_shift", "ln2_scale", "ln2_shift")):
                    load(sp, ln_cols[:, i:i + 1], din["L0_ffn_" + n].rearrange("(c a) -> c a", a=1))
                load(sp, bv_row[:, :], across("L0_attn_bv"))
                load(sp, bo_row[0][:, :], across("L0_attn_bp"))
                load(sp, bo_row[1][:, :], across("L0_ffn_bo"))
                load(sp, gate[:, :], din["L0_ffn_gate_w"])
                load(sp, w1[:, :, :], din["L0_ffn_w1"].rearrange("e c h -> c e h"))
                load(sp, w2[:, :, :], din["L0_ffn_w2"].rearrange("e c h -> c e h"))
                load(sp, w3[:, :, :, :].rearrange("c e a d -> c (e a) d"),
                     din["L0_ffn_w3"].rearrange("e (a c) d -> c (e a) d", a=HALVES))
                sp.wait_ge(setup_step, 5)
                for v in range(2):
                    sp.dma_start(band_bounce[v].rearrange("r h m -> h r m"),
                                 band[:, v, :].unsqueeze(1).broadcast_to([H, P, BAND])).then_inc(band_written, 16)
                sp.wait_ge(band_written, 32)
                pitch = H * BAND
                for v, dst in ((0, bias_whole), (1, bias_qk[:, :, :])):
                    sp.dma_start(dst, bass.AP(tensor=band_bounce.tensor,
                                              offset=band_bounce.offset + v * P * pitch + P - 1,
                                              ap=[[pitch - 1, P], [BAND, H], [1, NEAR]])).then_inc(band_read, 16)

            total_loads = n_loads[0]

            @block.tensor
            def _(pe):
                pe.wait_ge(setup_step, 3)
                for v in range(2):
                    mm = nc.tensor.matmul(single[v][0:H, 0:BAND], table[:, :], onehot[:, v, :], start=True, stop=True)
                mm.then_inc(setup_mm, 1)

            @block.vector
            def _(dve):
                nc.vector.memset(table[BUCKETS:BUCKETS + 1, :], MASKED).then_inc(setup_step, 1)
                nc.vector.memset(minus_half[:, :], -0.5).then_inc(setup_step, 1)
                dve.wait_ge(loaded, 16 * total_loads)
                nc.vector.tensor_tensor(table[0:BUCKETS, :], table[0:BUCKETS, :], table_far[:, :],
                                        ALU.subtract).then_inc(setup_step, 1)
                dve.wait_ge(setup_mm, 1)
                for v in range(2):
                    nc.vector.tensor_copy(band[:, v, :], single[v][0:H, 0:BAND]).then_inc(setup_step, 1)
                nc.vector.tensor_copy(eye_bf[:, :], eye[:, :])
                nc.vector.tensor_copy(mask_kq[:, :], mask_f[:, 0, :])
                nc.vector.tensor_copy(mask_qk[:, :], mask_f[:, 1, :])
                nc.vector.tensor_copy(expert_rows[:, :], expert_rows_f[:, :])
                dve.wait_ge(band_read, 32)
                n = 5
                for part in range(3):
                    nc.vector.tensor_copy(bias_kq[:, part, :, :], bias_whole).then_inc(setup_step, 1)
                    n += 1
                    if part < 2:
                        dve.wait_ge(setup_step, n)
                        nc.vector.tensor_tensor(bias_whole, bias_whole, bias_kq[:, part, :, :], ALU.subtract).then_inc(setup_step, 1)
                        n += 1
                        dve.wait_ge(setup_step, n)

            @block.gpsimd
            def _(pool):
                for l in range(2):
                    nc.gpsimd.memset(k_stack[l][:, :, :], 1.0)
                for l in range(2):
                    nc.gpsimd.memset(v_aug[l][:, :, :, :], 0.0).then_inc(pool_step, 1)
                pool.wait_ge(pool_step, 2)
                for l in range(2):
                    nc.gpsimd.memset(v_aug[l][:, :, :, D:D + 1], 1.0)

        nc.all_engine_barrier(sems_to_clear=all_sems)

        def consumed(step):
            kind, a = step[0], step[1:]
            if kind == "max":
                return heads_maxed[a[0]], heads_by(a[1], a[2]) if a[0] == 0 else nth(*step)
            if kind == "exp":
                return exp_done[a[0]], nth(*step)
            if kind == "turn_max":
                return m_copied[a[0]], a[1] + 1
            if kind == "context":
                return ctx_ready[a[0]], 2 * a[1] + 2
            if kind in ("up", "widen"):
                return {"up": hidden_ready, "widen": weight_bc_ready}[kind], a[0] + 1
            if kind in ("gate", "turn_weights", "finish"):
                return {"gate": gate_read, "turn_weights": weight_copied, "finish": moe_read}[kind], 1
            return {"context_back": ctx_copied, "attended": y_read, "to_channels": hT_ready, "project_k": k_read,
                    "project_q": q_read, "project_v": v_ready}[kind][a[0]], 1

        def run(older, newer):
            steps = body_steps(older is not None, newer is not None)
            uses = [s for s in steps if s[0] in RING_KINDS]

            def slot_of(step):
                return ring[uses.index(step) % RING]

            with nc.Block() as block:
                @block.sync
                def _(sp):
                    if newer is not None:
                        sp.dma_start(x[:, :, :], din["L0_attn_x"][bass.ds(newer, 1), :, :].rearrange(
                            "a (t p) c -> p (a t) c", p=P)).then_inc(x_loaded, 16)

                    def stack_rows(parts, repeat, split, bounce, bounced, stack, rows):
                        sp.wait_ge(split, 1)
                        slot = 0
                        for n in (3, 2, 1):
                            part = 3 - n
                            for e in range(2):
                                half = slice(64 * e, 64 * e + 64)
                                src = parts[half, part:part + 1, :].broadcast_to([64, n, T]) if repeat else parts[half, 0:n, :]
                                dst = bounce[e, slot * D:(slot + n) * D, :].rearrange(
                                    "(s d) (p n) -> (d p) s n", s=n, p=PAIRS)
                                sp.dma_start(dst, src).then_inc(bounced, 16)
                            slot += n
                        sp.wait_ge(bounced, 16 * 6)
                        for e in range(2):
                            sp.dma_start(stack[64 * e:64 * e + ROWS, :, :].rearrange("r p n -> r (p n)"),
                                         bounce[e]).then_inc(rows, 16)

                    def split(l):
                        stack_rows(k_parts, False, k_split[l], k_bounce[l], k_bounced[l], k_stack[l], k_rows[l])
                        stack_rows(q_parts, True, q_split[l], q_bounce[l], q_bounced[l], q_stack[l], q_rows[l])

                    def turn_max(l, g):
                        sp.wait_ge(m_copied[l], g + 1)
                        sp.dma_start(m_bounce[l][g].rearrange("e t (p n) -> (e t p) n", p=GP),
                                     m_rows[:, g % 2, :]).then_inc(m_bounced[l][g], 16)
                        sp.wait_ge(m_bounced[l][g], 16)
                        for e in range(2):
                            r = 64 * e + ROWS
                            sp.dma_start(q_stack[l][r:r + MROWS, GP * g:GP * g + GP, :].rearrange("r p n -> r (p n)"),
                                         m_bounce[l][g, e]).then_inc(m_in_stack[l][g], 16)

                    for s in steps:
                        if s[0] == "turn_max":
                            turn_max(*s[1:])
                        elif s[0] == "split":
                            split(s[1])
                    if newer is not None:
                        sp.wait_ge(k_rows[1], 32)
                        sp.wait_ge(q_rows[1], 32)
                    if older is not None:
                        sp.wait_ge(result_ready, NT)
                        sp.dma_start(out[bass.ds(older, 1), :, :].rearrange("a (t p) c -> p (a t) c", p=P),
                                     result[:, :, :]).then_inc(stored, 16)
                        sp.wait_ge(stored, 16)

                @block.tensor
                def _(pe):
                    mm = nc.tensor.matmul

                    def claim(step):
                        i = uses.index(step)
                        if i >= RING:
                            pe.wait_ge(*consumed(uses[i - RING]))
                        return ring[i % RING]

                    def to_channels(slot, l):
                        pe.wait_ge(normed_ready[l], NT)
                        for t in range(NT):
                            ins = nc.tensor.transpose(slot[:, 0, P * t:P * t + P], normed[l // 2][:, t, :], eye[:, :])
                        ins.then_inc(normed_turned[l], 1)

                    def project_k(slot, l):
                        pe.wait_ge(hT_ready[l], 1)
                        ins = mm(slot[:, 0, :], wk[l][:, :], hT[0][:, :], start=True, stop=True)
                        if l == 0:
                            ins = mm(slot[:, 1, :], wk_rot[:, :], hT[0][:, :], start=True, stop=True)
                        ins.then_inc(k_proj[l], 1)

                    def project_q(slot, l):
                        ins = mm(slot[:, 0, :], wq[l][:, :], hT[0][:, :], start=True, stop=True)
                        if l == 0:
                            ins = mm(slot[:, 1, :], wq_rot[:, :], hT[0][:, :], start=True, stop=True)
                        ins.then_inc(q_proj[l], 1)

                    def project_v(slot, l):
                        for t in range(NT):
                            ins = mm(slot[:, 0, P * t:P * t + P], hT[0][:, P * t:P * t + P], wv[l][:, :], start=True, stop=True)
                        ins.then_inc(v_proj[l], 1)

                    def max_piece(slot, l, g, n):
                        if l == 0 and g == 0 and n == 0:
                            pe.wait_ge(k_rows[0], 32)
                            pe.wait_ge(q_rows[0], 32)
                        tile, pair0, pairs = MAX_PIECES[n]
                        keys = P * (tile + 1)
                        for pr in range(pairs):
                            pair = GP * g + pair0 + pr
                            for e in range(2):
                                rows = slice(64 * e, 64 * e + ROWS)
                                ins = mm(slot[:, e, keys * pr:keys * (pr + 1)],
                                         q_stack[l][rows, pair, P * tile:P * tile + P], k_stack[l][rows, pair, 0:keys],
                                         start=True, stop=(l == 0))
                            if l == 1:
                                for e in range(2):
                                    ins = mm(slot[:, e, keys * (pr + 1) - P:keys * (pr + 1)], eye_bf[:, :],
                                             mask_qk[:, :], start=False, stop=True)
                        ins.then_inc(max_scores[l], 1)

                    def turn_max(slot, l, g):
                        pe.wait_ge(m_split[l], g + 1)
                        view = slot[:, 0, :].bitcast(BF16)
                        for t in range(NT):
                            ins = nc.tensor.transpose(view[0:2 * MROWS * GP, P * t:P * t + P],
                                                      m_parts[:, g, t, :, :, :].rearrange("p e t q -> p (e t q)"),
                                                      eye_bf[:, :])
                        ins.then_inc(m_turned[l], 1)

                    def exp_piece(slot, l, g, n):
                        tile, pair0, pairs = EXP_PIECES[n]
                        queries = T - P * tile
                        near = min(NEAR, queries)
                        if n == 0:
                            pe.wait_ge(m_in_stack[l][g], 32)
                        for pr in range(pairs):
                            pair = GP * g + pair0 + pr
                            for e in range(2):
                                rows = slice(64 * e, 64 * e + ROWS + MROWS)
                                mm(slot[:, e, queries * pr:queries * (pr + 1)],
                                   k_stack[l][rows, pair, P * tile:P * tile + P], q_stack[l][rows, pair, P * tile:T],
                                   start=True, stop=False)
                            for e in range(2):
                                if l == 0:
                                    for part in range(3):
                                        ins = mm(slot[:, e, queries * pr:queries * pr + near], eye_bf[:, :],
                                                 bias_kq[:, part, 2 * pair + e, 0:near], start=False, stop=(part == 2))
                                else:
                                    ins = mm(slot[:, e, queries * pr:queries * pr + P], eye_bf[:, :], mask_kq[:, :],
                                             start=False, stop=True)
                        ins.then_inc(exp_scores[l], 1)

                    def values(l, g, kt):
                        acc = single[g % 2]
                        last = {0: 1, 1: 3, 2: 4, 3: 5}[kt]
                        pe.wait_ge(exp_done[l], nth("exp", l, g, last))
                        if kt == 0 and g >= 2:
                            pe.wait_ge(ctxT_copied[l], g - 1)
                        queries = T - P * kt
                        for j in range(GH):
                            ins = mm(acc[VCOL * j:VCOL * j + VCOL, P * kt:T], v_aug[l][:, kt, GH * g + j, :],
                                     probs[:, (NT * g + kt) % PBUF, j, 0:queries], start=(kt == 0), stop=(kt == NT - 1))
                        ins.then_inc(values_done[l], 1)

                    def context(slot, l, k):
                        pe.wait_ge(ctxT_copied[l], GROUPS)
                        for i in range(2):
                            t = 2 * k + i
                            for g in range(GROUPS):
                                ins = nc.tensor.transpose(slot[:, i, P * g:P * g + P], ctxT[:, g, P * t:P * t + P], eye[:, :])
                            ins.then_inc(ctx_turned[l], 1)

                    def context_back(slot, l):
                        for t in range(NT):
                            pe.wait_ge(ctx_ready[l], t + 1)
                            ins = nc.tensor.transpose(slot[:, 0, P * t:P * t + P], ctx_tok[:, t, :], eye[:, :])
                        ins.then_inc(ctx_back[l], 1)

                    def attended(slot, l):
                        pe.wait_ge(ctx_copied[l], 1)
                        for t in range(NT):
                            ins = mm(slot[:, 0, P * t:P * t + P], ctx_ch[:, P * t:P * t + P], wo[l][:, :], start=True, stop=True)
                        ins.then_inc(y_ready[l], 1)

                    def gate_scores(slot):
                        pe.wait_ge(hT_ready[2], 1)
                        for t in range(NT):
                            ins = mm(slot[:, 0, EXPERTS * t:EXPERTS * t + EXPERTS], hT[1][:, P * t:P * t + P], gate[:, :],
                                     start=True, stop=True)
                        ins.then_inc(gate_ready, 1)

                    def turn_weights(slot):
                        pe.wait_ge(weight_split, 1)
                        view = slot[:, 0, :].bitcast(BF16)
                        for t in range(NT):
                            ins = nc.tensor.transpose(view[0:3 * EXPERTS, P * t:P * t + P],
                                                      weight_parts[:, t, :, :].rearrange("p s e -> p (s e)"), eye_bf[:, :])
                        ins.then_inc(weight_turned, 1)

                    def up(slot, i):
                        e, a = i // HALVES, i % HALVES
                        mm(slot[:, 0, :], w1[:, e, P * a:P * a + P], hT[1][:, :], start=True, stop=True)
                        mm(slot[:, 1, :], w2[:, e, P * a:P * a + P], hT[1][:, :], start=True, stop=True).then_inc(up_ready, 1)

                    def widen(slot, e):
                        if e == 0:
                            pe.wait_ge(weight_copied, 1)
                        mm(slot[:, 0, :], expert_rows[:, P * e:P * e + P], weight_rows[:, :], start=True,
                           stop=True).then_inc(weight_wide, 1)

                    def down(i):
                        e, a = i // HALVES, i % HALVES
                        if i == 0 and newer is not None:
                            pe.wait_ge(ctxT_copied[0], GROUPS)
                        pe.wait_ge(hidden_w_ready, i + 1)
                        mm(single[0][:, :], w3[:, e, a, :], hidden_w[:, i % EBUF, :], start=(i == 0),
                           stop=(i == UNITS - 1)).then_inc(down_done, 1)

                    def finish(slot):
                        pe.wait_ge(moe_copied, 1)
                        for t in range(NT):
                            ins = nc.tensor.transpose(slot[:, 0, P * t:P * t + P], moe_ch[:, P * t:P * t + P], eye[:, :])
                        ins.then_inc(moe_turned, 1)

                    parts = {"to_channels": to_channels, "project_k": project_k, "project_q": project_q, "project_v": project_v,
                             "max": max_piece, "turn_max": turn_max, "exp": exp_piece, "values": values, "context": context,
                             "context_back": context_back, "attended": attended, "gate": gate_scores,
                             "turn_weights": turn_weights, "up": up, "widen": widen, "down": down, "finish": finish}
                    for s in steps:
                        if s[0] in RING_KINDS:
                            parts[s[0]](claim(s), *s[1:])
                        elif s[0] in parts:
                            parts[s[0]](*s[1:])

                @block.scalar
                def _(act):
                    def to_channels(slot, l):
                        act.wait_ge(normed_turned[l], 1)
                        if l == 0:
                            nc.scalar.activation(hT[0][:, :], slot[:, 0, :], ACT.Copy).then_inc(hT_ready[0], 1)
                        else:
                            col = 2 * (l - 1)
                            nc.scalar.activation(hT[l - 1][:, :], slot[:, 0, :], ACT.Identity, bias=ln_cols[:, col + 1:col + 2],
                                                 scale=ln_cols[:, col:col + 1]).then_inc(hT_ready[l], 1)

                    def project_k(slot, l):
                        if l == 1:
                            act.wait_ge(k_proj[1], 1)
                            nc.scalar.activation(qk_f[:, 0, :], slot[:, 0, :], ACT.Copy).then_inc(k_read[1], 1)

                    def project_q(slot, l):
                        if l == 1:
                            act.wait_ge(q_proj[1], 1)
                            nc.scalar.activation(qk_f[:, 1, :], slot[:, 0, :], ACT.Copy).then_inc(q_read[1], 1)

                    def turn_max(slot, l, g):
                        act.wait_ge(m_turned[l], g + 1)
                        if g >= 2:
                            act.wait_ge(m_bounced[l][g - 2], 16)
                        elif l == 0 and older is not None:
                            act.wait_ge(m_bounced[1][g + 2], 16)
                        view = slot[:, 0, :].bitcast(BF16)
                        nc.scalar.activation(m_rows[:, g % 2, :], view[0:2 * MROWS * GP, 0:T], ACT.Copy).then_inc(m_copied[l], 1)

                    def exp_piece(slot, l, g, i):
                        tile, pair0, pairs = EXP_PIECES[i]
                        queries = T - P * tile
                        buf = probs[:, (NT * g + tile) % PBUF, :, :]
                        act.wait_ge(exp_scores[l], nth("exp", l, g, i))
                        before = NT * g + tile - PBUF
                        if pair0 == 0 and before >= 0:
                            act.wait_ge(values_done[l], nth("values", l, before // NT, before % NT))
                        elif pair0 == 0 and l == 0 and older is not None:
                            act.wait_ge(values_done[1], GROUPS * NT)
                        src = slot[:, :, 0:queries * pairs].rearrange("p e (r q) -> p e r q", r=pairs)
                        dst = buf[:, 2 * pair0:2 * pair0 + 2 * pairs, 0:queries].rearrange("p (r e) q -> p e r q", e=2)
                        if pairs == 1:
                            src, dst = src[:, :, 0, :], dst[:, :, 0, :]
                        nc.scalar.activation(dst, src, ACT.Exp, scale=SCALE).then_inc(exp_done[l], 1)

                    def values(l, g, kt):
                        if kt == NT - 1:
                            if g == 0 and l == 0 and older is not None:
                                act.wait_ge(ctx_turned[1], NT)
                            act.wait_ge(values_done[l], nth("values", l, g, kt))
                            nc.scalar.activation(ctxT[:, g, :], single[g % 2][:, :], ACT.Copy).then_inc(ctxT_copied[l], 1)

                    def context_back(slot, l):
                        act.wait_ge(ctx_back[l], 1)
                        nc.scalar.activation(ctx_ch[:, :], slot[:, 0, :], ACT.Copy).then_inc(ctx_copied[l], 1)

                    def gate_scores(slot):
                        act.wait_ge(gap_ready, 1)
                        nc.scalar.activation(gap_exp[:, :], gap[:, :], ACT.Exp).then_inc(gap_exp_ready, 1)

                    def turn_weights(slot):
                        act.wait_ge(weight_turned, 1)
                        nc.scalar.activation(weight_rows[:, :], slot[:, 0, :].bitcast(BF16)[0:3 * EXPERTS, 0:T],
                                             ACT.Copy).then_inc(weight_copied, 1)

                    def up(slot, i):
                        act.wait_ge(up_ready, i + 1)
                        if i >= EBUF:
                            act.wait_ge(gated_ready, i - EBUF + 1)
                        nc.scalar.activation(tanh_t[:, i % EBUF, :], slot[:, 0, :], ACT.Tanh, scale=0.5).then_inc(tanh_ready, 1)

                    def widen(slot, e):
                        act.wait_ge(weight_wide, e + 1)
                        if e >= 2:
                            act.wait_ge(hidden_w_ready, HALVES * (e - 1))
                        nc.scalar.activation(weight_bc[:, e % 2, :], slot[:, 0, :], ACT.Copy, scale=0.5).then_inc(weight_bc_ready, 1)

                    def finish(slot):
                        act.wait_ge(down_done, UNITS)
                        nc.scalar.activation(moe_ch[:, :], single[0][:, :], ACT.Copy).then_inc(moe_copied, 1)

                    parts = {"to_channels": to_channels, "project_k": project_k, "project_q": project_q, "turn_max": turn_max,
                             "exp": exp_piece, "values": values, "context_back": context_back, "gate": gate_scores,
                             "turn_weights": turn_weights, "up": up, "widen": widen, "finish": finish}
                    for s in steps:
                        if s[0] in parts:
                            parts[s[0]](*([slot_of(s)] if s[0] in RING_KINDS else []), *s[1:])

                def split3(engine, whole, rest, parts, step, last):
                    step(engine.tensor_copy(parts[0], whole))
                    step(engine.tensor_tensor(rest, whole, parts[0], ALU.subtract))
                    step(engine.tensor_copy(parts[1], rest))
                    engine.tensor_tensor(parts[2], rest, parts[1], ALU.subtract).then_inc(last, 1)

                @block.gpsimd
                def _(pool):
                    steps_done = [0]

                    def step(ins):
                        steps_done[0] += 1
                        ins.then_inc(pool_step, 1)
                        pool.wait_ge(pool_step, steps_done[0])

                    def stats(n):
                        pool.wait_ge(var_ready[n], 1)
                        nc.gpsimd.tensor_tensor(rstd[:, n, :], var_eps[:, n, :], minus_half[:, :], ALU.pow).then_inc(rstd_ready[n], 1)

                    def split(l):
                        if l == 0:
                            pool.wait_ge(q_read[0], 1)
                            step(nc.gpsimd.tensor_tensor(qk_f[:, 1, :], rope_a[:, 1, :], rope_b[:, 1, :], ALU.add))
                        else:
                            pool.wait_ge(q_read[1], 1)
                            pool.wait_ge(q_bounced[0], 96)
                        split3(nc.gpsimd, qk_f[:, 1, :], qk_rest[:, 1, :], [q_parts[:, i, :] for i in range(3)], step, q_split[l])

                    def turn_max(l, g):
                        pool.wait_ge(group_max[l], g + 1) if l == 0 else pool.wait_ge(heads_maxed[1], nth("max", 1, g, 5))
                        shape = lambda i: m_parts[:, g, :, :, i, :].rearrange("p t e r -> p t r e")
                        view = lambda m: m[:, g, :, :].rearrange("p t (r e) -> p t r e", e=2)
                        split3(nc.gpsimd, view(neg_max), view(m_rest), [shape(i) for i in range(3)], step, m_split[l])

                    def up(i):
                        pool.wait_ge(hidden_ready, i + 1)
                        pool.wait_ge(weight_bc_ready, i // HALVES + 1)
                        if i >= EBUF:
                            pool.wait_ge(down_done, i - EBUF + 1)
                        nc.gpsimd.tensor_tensor(hidden_w[:, i % EBUF, :], hidden[:, i % EBUF, :],
                                                weight_bc[:, (i // HALVES) % 2, :], ALU.mult).then_inc(hidden_w_ready, 1)

                    if older is not None:
                        nc.gpsimd.tensor_copy(x1_older[:, :, :], x1[:, :, :]).then_inc(x1_kept, 1)
                    parts = {"stats": stats, "split": split, "turn_max": turn_max, "up": up}
                    for s in steps:
                        if s[0] in parts:
                            parts[s[0]](*s[1:])

                @block.vector
                def _(dve):
                    steps_done, nears = [0], [0]

                    def step(ins):
                        steps_done[0] += 1
                        ins.then_inc(vector_step, 1)
                        dve.wait_ge(vector_step, steps_done[0])

                    normed_by = {0: (x, None, 0), 1: (branch, x1, None), 2: (x1, u, None), 3: (u, None, 1),
                                 4: (u2, None, 2), 5: (branch, result, None)}

                    def stats(n):
                        src = normed_by[n][0]
                        if n == 0:
                            dve.wait_ge(x_loaded, 16)
                        if n == 1 and older is not None:
                            dve.wait_ge(x1_kept, 1)
                        for t in range(NT):
                            ins = nc.vector.bn_stats(stats_t[:, t, :], src[:, t, :])
                        step(ins)
                        for t in range(NT):
                            ins = nc.vector.bn_aggr(mean_var[:, n, t, :], stats_t[:, t, :])
                        step(ins)
                        nc.vector.tensor_scalar(var_eps[:, n, :], mean_var[:, n, :, 1], EPS, None, ALU.add).then_inc(var_ready[n], 1)

                    def norm(n):
                        src, dst, stage = normed_by[n]
                        if stage is not None:
                            dst = normed[stage // 2]
                        dve.wait_ge(rstd_ready[n], 1)
                        for t in range(NT):
                            ins = nc.vector.tensor_scalar(dst[:, t, :], src[:, t, :], mean_var[:, n, t, 0:1], rstd[:, n, t:t + 1],
                                                          ALU.subtract, ALU.mult)
                            if stage is not None:
                                ins.then_inc(normed_ready[stage], 1)
                        if stage is None:
                            step(ins)
                        if n == 1:
                            step(nc.vector.tensor_tensor(x1[:, :, :], x1[:, :, :], x[:, :, :], ALU.add))
                        if n == 5:
                            for t in range(NT):
                                nc.vector.tensor_tensor(result[:, t, :], result[:, t, :], x1_older[:, t, :], ALU.add).then_inc(result_ready, 1)

                    def project(i, slot, proj, read):
                        col = 2 - 2 * i
                        dve.wait_ge(proj, 1)
                        nc.vector.scalar_tensor_tensor(rope_a[:, i, :], slot[:, 0, :], bias_cols[:, col:col + 1], cos_t[:, :],
                                                       ALU.add, ALU.mult)
                        nc.vector.scalar_tensor_tensor(rope_b[:, i, :], slot[:, 1, :], bias_cols[:, col + 1:col + 2],
                                                       sin_t[:, :], ALU.add, ALU.mult).then_inc(read, 1)

                    def project_k(slot, l):
                        if l == 0:
                            project(0, slot, k_proj[0], k_read[0])

                    def project_q(slot, l):
                        if l == 0:
                            project(1, slot, q_proj[0], q_read[0])

                    def project_v(slot, l):
                        dve.wait_ge(v_proj[l], 1)
                        src = slot[:, 0, :].rearrange("p (t h d) -> p t h d", t=NT, h=H)
                        for t in range(NT):
                            if l == 0:
                                ins = nc.vector.tensor_tensor(v_aug[l][:, t, :, 0:D], src[:, t, :, :],
                                                              bv_row[:, :].rearrange("p (h d) -> p h d", h=H), ALU.add)
                            else:
                                ins = nc.vector.tensor_copy(v_aug[l][:, t, :, 0:D], src[:, t, :, :])
                        ins.then_inc(v_ready[l], 1)

                    def split(l):
                        dve.wait_ge(k_read[l], 1)
                        if l == 0:
                            step(nc.vector.tensor_tensor(qk_f[:, 0, :], rope_a[:, 0, :], rope_b[:, 0, :], ALU.add))
                        else:
                            dve.wait_ge(k_bounced[0], 96)
                        split3(nc.vector, qk_f[:, 0, :], qk_rest[:, 0, :], [k_parts[:, i, :] for i in range(3)], step, k_split[l])

                    def max_piece(slot, l, g, n):
                        tile, pair0, pairs = MAX_PIECES[n]
                        keys = P * (tile + 1)
                        heads = 2 * pairs
                        h0 = GH * g + 2 * pair0
                        dve.wait_ge(max_scores[l], nth("max", l, g, n))
                        if l == 0 and n == 0 and older is not None:
                            dve.wait_ge(m_split[1], g + 1)
                        scores = slot[:, :, 0:keys * pairs].rearrange("p e (r k) -> p e r k", r=pairs)
                        if pairs == 1:
                            scores = scores[:, :, 0, :]
                        if l == 1:
                            dst = neg_max[:, g, tile, 2 * pair0:2 * pair0 + heads].rearrange("p (r e) -> p e r", e=2)
                            if pairs == 1:
                                dst = dst[:, :, 0]
                            nc.vector.tensor_reduce(dst, scores, AX_X, ALU.max, negate=True).then_inc(heads_maxed[1], 1)
                            return
                        if tile >= 2:
                            nc.vector.tensor_reduce(far_max[:, tile, h0:h0 + heads], scores[:, :, 0:keys - NEAR], AX_X, ALU.max)
                        near = min(NEAR, keys)
                        for r in range(pairs):
                            for e in range(2):
                                h = h0 + 2 * r + e
                                if nears[0] >= NBUF:
                                    dve.wait_ge(heads_maxed[0], nears[0] - NBUF + 1)
                                nc.vector.tensor_tensor_reduce(
                                    out=near_sum[:, nears[0] % NBUF, 0:near], in0=slot[:, e, keys * (r + 1) - near:keys * (r + 1)],
                                    in1=bias_qk[:, h, NEAR - near:NEAR], scale=1.0, scalar=2.0 * MASKED, op0=ALU.add, op1=ALU.max,
                                    accum_out=near_max[:, tile, h:h + 1]).then_inc(heads_maxed[0], 1)
                                nears[0] += 1
                        if n == len(MAX_PIECES) - 1:
                            dve.wait_ge(heads_maxed[0], nears[0])
                            hs = slice(GH * g, GH * g + GH)
                            nc.vector.tensor_scalar(neg_max[:, g, 0:2, :], near_max[:, 0:2, hs], -1.0, None, ALU.mult)
                            step(nc.vector.tensor_tensor(m_most[:, g, 2:NT, :], near_max[:, 2:NT, hs], far_max[:, 2:NT, hs], ALU.max))
                            nc.vector.tensor_scalar(neg_max[:, g, 2:NT, :], m_most[:, g, 2:NT, :], -1.0, None,
                                                    ALU.mult).then_inc(group_max[l], 1)

                    def context(slot, l, k):
                        for i in range(2):
                            t = 2 * k + i
                            dve.wait_ge(ctx_turned[l], t + 1)
                            src = slot[:, i, :].rearrange("p (h v) -> p h v", h=H)
                            step(nc.vector.reciprocal(row_inv[:, t, :], src[:, :, D]))
                            nc.vector.tensor_tensor(ctx_tok[:, t, :].rearrange("p (h d) -> p h d", h=H), src[:, :, 0:D],
                                                    row_inv[:, t, :].unsqueeze(2).broadcast_to([P, H, D]),
                                                    ALU.mult).then_inc(ctx_ready[l], 1)

                    def attended(slot, l):
                        dve.wait_ge(y_ready[l], 1)
                        dst = branch if l == 0 else u2
                        nc.vector.tensor_tensor(dst[:, :, :], slot[:, 0, :].rearrange("p (t c) -> p t c", t=NT),
                                                bo_row[l][:, :].unsqueeze(1).broadcast_to([P, NT, C]), ALU.add).then_inc(y_read[l], 1)
                        dve.wait_ge(y_read[l], 1)
                        if l == 1:
                            step(nc.vector.tensor_tensor(u2[:, :, :], u2[:, :, :], u[:, :, :], ALU.add))

                    def gate_scores(slot):
                        dve.wait_ge(gate_ready, 1)
                        nc.vector.tensor_copy(gate_s[:, :, :], slot[:, 0, 0:NT * EXPERTS].rearrange(
                            "p (t e) -> p t e", t=NT)).then_inc(gate_read, 1)
                        dve.wait_ge(gate_read, 1)
                        for t in range(NT):
                            ins = nc.vector.max(top8[:, t, :], gate_s[:, t, :])
                        step(ins)
                        nc.vector.tensor_tensor(gap[:, :], top8[:, :, 1], top8[:, :, 0], ALU.subtract).then_inc(gap_ready, 1)
                        for t in range(NT):
                            ins = nc.vector.max_index(top_ids[:, t, :], top8[:, t, :], gate_s[:, t, :])
                        step(ins)
                        step(nc.vector.tensor_copy(top_ids_f[:, :, :], top_ids[:, :, 0:2]))

                    def turn_weights(slot):
                        dve.wait_ge(gap_exp_ready, 1)
                        step(nc.vector.tensor_scalar(gap_den[:, :], gap_exp[:, :], 1.0, None, ALU.add))
                        step(nc.vector.reciprocal(top_p[:, 0, :], gap_den[:, :]))
                        step(nc.vector.tensor_tensor(top_p[:, 1, :], top_p[:, 0, :], gap_exp[:, :], ALU.mult))
                        for k in range(2):
                            ins = nc.vector.tensor_tensor(pick[:, k, :, :], expert_ids[:, :, :],
                                                          top_ids_f[:, :, k].unsqueeze(2).broadcast_to([P, NT, EXPERTS]), ALU.is_equal)
                        step(ins)
                        for k in range(2):
                            ins = nc.vector.tensor_tensor(pick_w[:, k, :, :], pick[:, k, :, :],
                                                          top_p[:, k, :].unsqueeze(2).broadcast_to([P, NT, EXPERTS]), ALU.mult)
                        step(ins)
                        step(nc.vector.tensor_tensor(weight[:, :, :], pick_w[:, 0, :, :], pick_w[:, 1, :, :], ALU.add))
                        split3(nc.vector, weight[:, :, :], weight_rest[:, 0, :, :],
                               [weight_parts[:, :, i, :] for i in range(3)], step, weight_split)

                    def up(slot, i):
                        dve.wait_ge(tanh_ready, i + 1)
                        nc.vector.scalar_tensor_tensor(gated[:, i % EBUF, :], tanh_t[:, i % EBUF, :], 1.0, slot[:, 0, :],
                                                       ALU.add, ALU.mult).then_inc(gated_ready, 1)
                        dve.wait_ge(gated_ready, i + 1)
                        if i >= EBUF:
                            dve.wait_ge(hidden_w_ready, i - EBUF + 1)
                        nc.vector.tensor_tensor(hidden[:, i % EBUF, :], gated[:, i % EBUF, :], slot[:, 1, :],
                                                ALU.mult).then_inc(hidden_ready, 1)

                    def finish(slot):
                        dve.wait_ge(moe_turned, 1)
                        nc.vector.tensor_tensor(branch[:, :, :], u2[:, :, :], slot[:, 0, :].rearrange("p (t c) -> p t c", t=NT),
                                                ALU.add).then_inc(moe_read, 1)
                        dve.wait_ge(moe_read, 1)

                    parts = {"stats": stats, "norm": norm, "project_k": project_k, "project_q": project_q, "project_v": project_v,
                             "split": split, "max": max_piece, "context": context, "attended": attended, "gate": gate_scores,
                             "turn_weights": turn_weights, "up": up, "finish": finish}
                    for s in steps:
                        if s[0] in parts:
                            parts[s[0]](*([slot_of(s)] if s[0] in RING_KINDS else []), *s[1:])

            nc.all_engine_barrier(sems_to_clear=all_sems)

        run(None, 0)
        with nc.Fori(0, B - 1) as b:
            run(b, b + 1)
        run(B - 1, None)


AS_GIVEN = ["L0_attn_x", "L0_attn_Wv", "L0_attn_bv", "L0_attn_Wp", "L0_attn_bp", "L0_attn_rel_bias_table",
            "L0_ffn_ln1_scale", "L0_ffn_ln1_shift", "L0_ffn_wv", "L0_ffn_wo", "L0_ffn_bo", "L0_ffn_ln2_scale",
            "L0_ffn_ln2_shift", "L0_ffn_gate_w", "L0_ffn_w1", "L0_ffn_w2", "L0_ffn_w3"]


def by_parity(w, partner=False):
    w = np.asarray(w)
    w = w.reshape(w.shape[:-1] + (PAIRS, 2, D))
    if partner:
        w = np.concatenate([w[..., D // 2:], w[..., :D // 2]], axis=-1)
    return np.moveaxis(w, -3, -1).reshape(w.shape[:-3] + (C,))


def kernel(**inputs):
    import concourse.bacc as bacc
    from concourse.bass_utils import run_bass_kernel_spmd

    laid_out = {name: inputs[name] for name in AS_GIVEN}
    laid_out["qk_weights"] = np.stack([
        by_parity(inputs["L0_attn_Wq"]), by_parity(inputs["L0_attn_Wk"]),
        by_parity(inputs["L0_ffn_wq"]), by_parity(inputs["L0_ffn_wk"]),
        by_parity(inputs["L0_attn_Wq"], True), by_parity(inputs["L0_attn_Wk"], True)])
    laid_out["qk_biases"] = np.stack([
        by_parity(inputs["L0_attn_bq"]), by_parity(inputs["L0_attn_bq"], True),
        by_parity(inputs["L0_attn_bk"]), by_parity(inputs["L0_attn_bk"], True)], axis=1)
    nc = bacc.Bacc("TRN2", target_bir_lowering=False, num_devices=1)
    arrays, din, const = {}, {}, {}
    for name, a in laid_out.items():
        a = np.ascontiguousarray(a)
        arrays[f"in_{name}"] = a
        din[name] = nc.dram_tensor(f"in_{name}", a.shape, mybir.dt.from_np(a.dtype), kind="ExternalInput").ap()
    for name, a in shape_constants().items():
        arrays[f"const_{name}"] = a
        const[name] = nc.dram_tensor(f"const_{name}", a.shape, F32, kind="ExternalInput").ap()
    out = nc.dram_tensor("out", (B, T, C), F32, kind="ExternalOutput").ap()
    sandwich(nc, din, const, out)
    r = run_bass_kernel_spmd(nc, [arrays], core_ids=[0])
    return r.results[0]["out"]
```

```python
from contextlib import ExitStack

import numpy as np

import concourse.bass as bass
from concourse import mybir

F32 = mybir.dt.float32
BF16 = mybir.dt.bfloat16
U32 = mybir.dt.uint32
ALU = mybir.AluOpType
ACT = mybir.ActivationFunctionType
AX_X = mybir.AxisListType.X

B, T, C = 16, 512, 128
H = 16
D = C // H
P = 128
NT = T // P
PAIRS = H // 2
GROUPS = 4
GH = H // GROUPS
GP = GH // 2
SCALE = float(1.0 / np.sqrt(D))
EPS = 1e-5
SLOTS = 6
ROWS = SLOTS * D
MROWS = 3
MAX_AT = 32
STACK = ROWS + MROWS
BUCKETS = 32
BAND = 384
NEAR = 2 * P
MASKED = -1e30
EXPERTS, HID = 8, 256
HALVES = HID // P
VCOL = 32
NORMS = 6
RING = 3
PBUF = 3
EBUF = 3
NBUF = 2

UNITS = EXPERTS * HALVES

MAX_PIECES = [(0, 0, 2), (1, 0, 2), (2, 0, 1), (2, 1, 1), (3, 0, 1), (3, 1, 1)]
EXP_PIECES = [(0, 0, 1), (0, 1, 1), (1, 0, 1), (1, 1, 1), (2, 0, 2), (3, 0, 2)]
VALUES_AFTER = {2: [(0, 0)], 4: [(0, 1)], 5: [(0, 2)], 0: [(1, 3)]}
LAST_VALUES_AFTER = {3: [(0, 0)], 5: [(0, 1)], 0: [(1, 3)]}
TURN_AT = 1

ADD_FROM = 3
ADDED_HEADS = H - GH * ADD_FROM


def attention_steps(layers):
    groups = [(l, g) for l in layers for g in range(GROUPS)]
    order = [("max", *groups[0], i) for i in range(6)]
    order += [("max", *groups[1], i) for i in range(3)] + [("turn_max", *groups[0])] + [("max", *groups[1], i) for i in range(3, 6)]
    for k in range(len(groups)):
        for i in range(len(EXP_PIECES)):
            if k + 2 < len(groups):
                order.append(("max", *groups[k + 2], i))
            order.append(("exp", *groups[k], i))
            after = LAST_VALUES_AFTER if k + 1 == len(groups) else VALUES_AFTER
            order += [("values", *groups[k - back], kt) for back, kt in after.get(i, ()) if k >= back]
            if i == TURN_AT and k + 1 < len(groups):
                order.append(("turn_max", *groups[k + 1]))
    return order + [("values", *groups[-1], kt) for kt in (2, 3)]


def expert_steps():
    order = [("widen", 0), ("up", 0), ("up", 1)]
    for i in range(2, UNITS):
        if i % HALVES == 0:
            order.append(("widen", i // HALVES))
        order.append(("up", i))
        order.append(("down", i - 2))
    return order + [("down", UNITS - 2), ("down", UNITS - 1)]


def projection_steps(l):
    split = [("split", l, i, stage) for stage in range(3) for i in range(2)]
    return [("to_channels", l), ("project_k", l), ("project_q", l)] + split[:2] + [("project_v", l)] + split[2:]


def output_steps(l):
    return [("context", l, 0), ("context", l, 1), ("context_back", l), ("attended", l)]


def insert(core, between, first, last):
    at = [first + (last - first) * k // max(len(between), 1) for k in range(len(between))]
    out = []
    for k, step in enumerate(core):
        out += [between[m] for m in range(len(between)) if at[m] == k and between[m]]
        out.append(step)
    return out


def body_steps(oldest, older, newer):
    finish = [("finish",), ("stats", 5), ("norm", 5)] if oldest else []
    first = [("stats", 0), ("norm", 0), None] + projection_steps(0)
    second = (output_steps(0) + [("stats", 1), ("norm", 1), ("stats", 2), ("norm", 2), ("stats", 3), ("norm", 3)]
              + 4 * [None] + projection_steps(1) + [("stack_in", 1, 0, GROUPS)])
    mixture = output_steps(1) + [("stats", 4), ("norm", 4), ("to_channels", 2), ("gate",), None, ("weigh",), None, ("turn_weights",)]
    experts = [("keep_x1",)] + expert_steps() + [("keep_experts",)]
    if not older:
        return finish + ([s for s in first if s] + [("stack_in", 0, g, 1) for g in range(GROUPS)] + attention_steps([0]) + [s for s in second if s] if newer else [])
    if not newer:
        return finish + attention_steps([1]) + [s for s in mixture if s] + experts
    core = attention_steps([1, 0])
    steps = insert(core, first, 1, core.index(("exp", 1, 0, 3)))
    steps = insert(steps, finish, steps.index(("exp", 1, 2, 0)), steps.index(("exp", 1, 3, 0)))
    steps = insert(steps, mixture, steps.index(("values", 1, GROUPS - 1, NT - 1)) + 1, steps.index(("exp", 0, 2, 0)))
    for g in range(GROUPS):
        steps.insert(steps.index(("exp", 1, max(g, 1), 5)) + 1 + (g == 1), ("stack_in", 0, g, 1))
    return steps + insert(experts, second, 1, int(0.7 * len(experts)))


RING_KINDS = ("max", "turn_max", "exp", "context", "context_back", "attended", "to_channels", "project_k", "project_q",
              "project_v", "gate", "turn_weights", "up", "widen", "finish")


def nth(kind, l, g, i):
    return [s for s in attention_steps([l]) if s[0] == kind].index((kind, l, g, i)) + 1


def heads_by(g, i):
    return sum(2 * MAX_PIECES[s[3]][2] for s in [s for s in attention_steps([0]) if s[0] == "max"][:nth("max", 0, g, i)])


def shape_constants():
    inv = 1.0 / 10000.0 ** (np.arange(0, D, 2, dtype=np.float32) / D)
    freqs = np.arange(T, dtype=np.float32)[:, None] * inv[None, :].astype(np.float32)
    freqs = np.concatenate([freqs, freqs], axis=-1)
    cos, sin = np.cos(freqs).T, np.sin(freqs).T
    sign = np.where(np.arange(D) < D // 2, -1.0, 1.0)[:, None]
    spread = lambda x: np.broadcast_to(x[None, :, None, :], (2, D, PAIRS, T)).reshape(P, T)
    n = np.arange(BAND) - (P - 1)
    exact = BUCKETS // 2
    far = exact + (np.log(np.maximum(n, 1).astype(np.float32) / exact) / np.log(128 / exact)
                   * (BUCKETS - exact)).astype(np.int32)
    bucket = np.where(n < exact, n, np.minimum(far, BUCKETS - 1))
    bucket = np.where(n < 0, BUCKETS, bucket)
    forward = (np.arange(BUCKETS + 1)[:, None] == bucket[None, :])
    eye = np.eye(P)
    causal = np.where(np.arange(P)[:, None] > np.arange(P)[None, :], MASKED, 0.0)
    experts = np.zeros((3, EXPERTS, EXPERTS, P))
    for e in range(EXPERTS):
        experts[:, e, e, :] = 1.0
    f = lambda x: np.ascontiguousarray(x, dtype=np.float32)
    return {
        "cos": f(spread(cos)), "sin": f(spread(sin * sign)),
        "band": f(forward),
        "eye": f(eye),
        "mask_kq": f(causal), "mask_qk": f(causal.T),
        "expert_rows": f(experts.reshape(3 * EXPERTS, EXPERTS * P)),
        "expert_ids": f(np.broadcast_to(np.arange(EXPERTS), (P, NT, EXPERTS))),
    }


def sandwich(nc, din, const, out):
    ctx = ExitStack()
    with ctx:
        def sb(name, shape, dt=F32):
            return ctx.enter_context(nc.sbuf_tensor(name, shape, dt))

        sems = []

        def sem(name):
            s = ctx.enter_context(nc.semaphore(name))
            sems.append(s)
            return s

        def sem2(name):
            return [sem(f"{name}{i}") for i in range(2)]

        def scratch(name, shape, dt):
            return nc.dram_tensor(name, shape, dt, kind="Internal").ap()

        q_bounce = [scratch(f"q_bounce{i}", [2, STACK, PAIRS * T], BF16) for i in range(2)]
        k_bounce = [scratch(f"k_bounce{i}", [2, STACK, PAIRS * T], BF16) for i in range(2)]
        band_bounce = scratch("band_bounce", [P, H, BAND], F32)

        cos_t, sin_t = sb("cos_t", [P, T]), sb("sin_t", [P, T])
        eye = sb("eye", [P, P])
        eye_bf = sb("eye_bf", [P, P], BF16)
        mask_kq, mask_qk = sb("mask_kq", [P, P], BF16), sb("mask_qk", [P, P], BF16)
        table = sb("table", [BUCKETS + 1, H])
        table_far = sb("table_far", [BUCKETS, H])
        bias_qk = sb("bias_qk", [P, H, NEAR])
        bias_kq = sb("bias_kq", [P, 3, H - ADDED_HEADS, NEAR], BF16)
        bias_added = sb("bias_added", [P, ADDED_HEADS, NEAR])
        expert_rows = sb("expert_rows", [3 * EXPERTS, EXPERTS * P], BF16)
        expert_ids = sb("expert_ids", [P, NT, EXPERTS])
        wq = [sb(f"wq{i}", [P, C]) for i in range(2)]
        wk = [sb(f"wk{i}", [P, C]) for i in range(2)]
        wv = [sb(f"wv{i}", [P, C]) for i in range(2)]
        wo = [sb(f"wo{i}", [P, C]) for i in range(2)]
        wq_rot, wk_rot = sb("wq_rot", [P, C]), sb("wk_rot", [P, C])
        bias_cols = sb("bias_cols", [P, 4])
        ln_cols = sb("ln_cols", [P, 4])
        bv_row, bo_row = sb("bv_row", [P, C]), [sb(f"bo_row{i}", [P, C]) for i in range(2)]
        gate = sb("gate", [P, EXPERTS])
        w1, w2 = sb("w1", [P, EXPERTS, HID]), sb("w2", [P, EXPERTS, HID])
        w3 = sb("w3", [P, EXPERTS, HALVES, C])
        minus_half = sb("minus_half", [P, NT])

        x = sb("x", [P, NT, C])
        x1, x1_older, u, u2, branch = (sb(n, [P, NT, C]) for n in ("x1", "x1_older", "u", "u2", "branch"))
        normed = [sb(f"normed{i}", [P, NT, C]) for i in range(2)]
        stats_t = sb("stats_t", [P, NT, 6])
        mean_var = sb("mean_var", [P, NORMS, NT, 2])
        var_eps = sb("var_eps", [P, NORMS, NT])
        rstd = sb("rstd", [P, NORMS, NT])
        hT = [sb(f"hT{i}", [P, T]) for i in range(2)]
        rope_a, rope_b = sb("rope_a", [P, 2, T]), sb("rope_b", [P, 2, T])
        qk_f = sb("qk_f", [P, 2, T])
        qk_rest = rope_a
        q_parts, k_parts = sb("q_parts", [P, 3, T], BF16), sb("k_parts", [P, 3, T], BF16)
        q_stack = sb("q_stack", [P, 2, PAIRS, T], BF16)
        k_stack = sb("k_stack", [P, PAIRS, T], BF16)
        v_aug = [sb(f"v_aug{i}", [P, NT, H, VCOL]) for i in range(2)]
        near_sum = sb("near_sum", [P, NBUF, NEAR])
        near_max, far_max = sb("near_max", [P, NT, H]), sb("far_max", [P, NT, H])
        neg_max = sb("neg_max", [P, GROUPS, NT, GH])
        m_rest = sb("m_rest", [P, GROUPS, NT, GH])
        m_most = sb("m_most", [P, GROUPS, NT, GH])
        m_parts = sb("m_parts", [P, 2, NT, GP, P], BF16)
        probs = sb("probs", [P, PBUF, GH, T])
        ctxT = sb("ctxT", [P, GROUPS, T])
        flat = probs[:, :, :, :].rearrange("p a b n -> p (a b n)")
        bias_whole = flat[:, 0:H * NEAR].rearrange("p (h m) -> p h m", h=H)
        onehot = flat[0:BUCKETS + 1, H * NEAR:H * NEAR + BAND]
        band = flat[0:H, H * NEAR + BAND:H * NEAR + 2 * BAND]
        expert_rows_f = ctxT[0:3 * EXPERTS, :, :].rearrange("p g n -> p (g n)")[:, 0:EXPERTS * P]
        mask_f = ctxT[:, GROUPS - 1, 0:2 * P].rearrange("p (v n) -> p v n", v=2)
        row_inv = sb("row_inv", [P, NT, H])
        ctx_tok = sb("ctx_tok", [P, NT, C])
        ctx_ch = rope_a[:, 0, :]
        gate_s = sb("gate_s", [P, NT, EXPERTS])
        top8 = sb("top8", [P, NT, EXPERTS])
        top_ids = sb("top_ids", [P, NT, EXPERTS], U32)
        top_ids_f = sb("top_ids_f", [P, NT, 2])
        gap = sb("gap", [P, NT])
        gap_exp = sb("gap_exp", [P, NT])
        gap_den = sb("gap_den", [P, NT])
        top_p = sb("top_p", [P, 2, NT])
        pick = sb("pick", [P, 2, NT, EXPERTS])
        pick_w = sb("pick_w", [P, 2, NT, EXPERTS])
        weight = sb("weight", [P, NT, EXPERTS])
        weight_rest = sb("weight_rest", [P, 2, NT, EXPERTS])
        weight_parts = sb("weight_parts", [P, NT, 3, EXPERTS], BF16)
        weight_rows = sb("weight_rows", [3 * EXPERTS, T], BF16)
        weight_bc = rope_b
        spare = probs[:, :, :, :].rearrange("p a b n -> p (a b) n")
        tanh_t, gated, hidden, hidden_w = (spare[:, EBUF * i:EBUF * (i + 1), :] for i in range(4))
        moe_ch = sb("moe_ch", [P, T])
        result = sb("result", [P, NT, C])

        ring = [ctx.enter_context(nc.psum_tensor(f"ring{i}", [P, 2, T], F32)) for i in range(RING)]
        single = [ctx.enter_context(nc.psum_tensor(f"single{i}", [P, T], F32)) for i in range(2)]

        table_loaded, loaded, setup_step, setup_mm = sem("table_loaded"), sem("loaded"), sem("setup_step"), sem("setup_mm")
        bias_turned, bias_copied = sem("bias_turned"), sem("bias_copied")
        stack_cleared, rows_written = sem("stack_cleared"), sem("rows_written")
        band_written, band_read = sem("band_written"), sem("band_read")
        x_loaded = sem("x_loaded")
        vector_step, pool_step = sem("vector_step"), sem("pool_step")
        var_ready, rstd_ready = ([sem(f"{n}{i}") for i in range(NORMS)] for n in ("var_ready", "rstd_ready"))
        normed_ready, normed_turned, hT_ready = ([sem(f"{n}{i}") for i in range(3)] for n in ("normed_ready", "normed_turned", "hT_ready"))
        k_proj, q_proj, v_proj = sem2("k_proj"), sem2("q_proj"), sem2("v_proj")
        k_read, q_read = sem2("k_read"), sem2("q_read")
        q_split, k_split, v_ready = sem2("q_split"), sem2("k_split"), sem2("v_ready")
        k_summed, q_summed, k_rounded, q_rounded = sem("k_summed"), sem("q_summed"), sem2("k_rounded"), sem2("q_rounded")
        k_rest_ready, q_rest_ready = sem2("k_rest_ready"), sem2("q_rest_ready")
        q_bounced, k_bounced = sem2("q_bounced"), sem2("k_bounced")
        stack_in = [[sem(f"stack_in0_{g}") for g in range(GROUPS)], [sem("stack_in1")]]
        max_scores, heads_maxed = sem2("max_scores"), sem2("heads_maxed")
        group_max, m_split = sem2("group_max"), sem2("m_split")
        m_turned, m_in_stack = sem2("m_turned"), sem2("m_in_stack")
        exp_scores, exp_done = sem2("exp_scores"), sem2("exp_done")
        bias_in = sem("bias_in")
        values_done, ctxT_copied = sem2("values_done"), sem2("ctxT_copied")
        ctx_turned, ctx_ready = sem2("ctx_turned"), sem2("ctx_ready")
        ctx_back, ctx_copied, y_ready, y_read = sem2("ctx_back"), sem2("ctx_copied"), sem2("y_ready"), sem2("y_read")
        x1_kept = sem("x1_kept")
        gate_ready, gate_read, gap_ready, gap_exp_ready = sem("gate_ready"), sem("gate_read"), sem("gap_ready"), sem("gap_exp_ready")
        weight_split, weight_turned, weight_copied = sem("weight_split"), sem("weight_turned"), sem("weight_copied")
        weight_wide, weight_bc_ready = sem("weight_wide"), sem("weight_bc_ready")
        up_ready, tanh_ready, gated_ready = sem("up_ready"), sem("tanh_ready"), sem("gated_ready")
        hidden_ready, hidden_w_ready = sem("hidden_ready"), sem("hidden_w_ready")
        down_done, moe_copied, moe_turned, moe_read = sem("down_done"), sem("moe_copied"), sem("moe_turned"), sem("moe_read")
        result_ready, stored = sem("result_ready"), sem("stored")
        all_sems = range(min(s.num for s in sems), max(s.num for s in sems) + 1)

        n_loads = [0]
        with nc.Block() as block:
            def load(eng, dst, src):
                n_loads[0] += 1
                eng.dma_start(dst, src).then_inc(loaded, 16)

            def across(name):
                v = din[name]
                return bass.AP(tensor=v.tensor, offset=v.offset, ap=[[0, P], [1, C]])

            @block.scalar
            def _(act):
                load(act, cos_t[:, :], const["cos"])
                load(act, sin_t[:, :], const["sin"])
                load(act, eye[:, :], const["eye"])
                load(act, mask_f[:, 0, :], const["mask_kq"])
                load(act, mask_f[:, 1, :], const["mask_qk"])
                load(act, expert_rows_f[:, :], const["expert_rows"])
                load(act, expert_ids[:, :, :], const["expert_ids"])
                for i, w in enumerate((wq[0], wk[0], wq[1], wk[1], wq_rot, wk_rot)):
                    load(act, w[:, :], din["qk_weights"][i])
                load(act, bias_cols[:, :], din["qk_biases"])
                load(act, wv[0][:, :], din["L0_attn_Wv"])
                load(act, wv[1][:, :], din["L0_ffn_wv"])
                load(act, wo[0][:, :], din["L0_attn_Wp"])
                load(act, wo[1][:, :], din["L0_ffn_wo"])
                for i, n in enumerate(("ln1_scale", "ln1_shift", "ln2_scale", "ln2_shift")):
                    load(act, ln_cols[:, i:i + 1], din["L0_ffn_" + n].rearrange("(c a) -> c a", a=1))
                load(act, bv_row[:, :], across("L0_attn_bv"))
                load(act, bo_row[0][:, :], across("L0_attn_bp"))
                load(act, bo_row[1][:, :], across("L0_ffn_bo"))
                load(act, gate[:, :], din["L0_ffn_gate_w"])
                load(act, w1[:, :, :], din["L0_ffn_w1"].rearrange("e c h -> c e h"))
                load(act, w2[:, :, :], din["L0_ffn_w2"].rearrange("e c h -> c e h"))
                load(act, w3[:, :, :, :].rearrange("c e a d -> c (e a) d"),
                     din["L0_ffn_w3"].rearrange("e (a c) d -> c (e a) d", a=HALVES))
                for h in range(0, H, 2):
                    act.wait_ge(bias_turned, h // 2 + 1)
                    nc.scalar.activation(bias_qk[:, h:h + 2, :].rearrange("p h m -> p (h m)"), ring[h // 2 % RING][:, 0, :],
                                         ACT.Copy).then_inc(bias_copied, 1)

            @block.sync
            def _(sp):
                tb = din["L0_attn_rel_bias_table"]
                sp.dma_start(onehot, const["band"]).then_inc(table_loaded, 16)
                sp.dma_start(table[0:BUCKETS, :], tb).then_inc(table_loaded, 16)
                sp.dma_start(table_far[:, :], bass.AP(tensor=tb.tensor, offset=tb.offset + (BUCKETS - 1) * H,
                                                      ap=[[0, BUCKETS], [1, H]])).then_inc(table_loaded, 16)
                sp.wait_ge(setup_step, 4)
                sp.dma_start(band_bounce.rearrange("r h m -> h r m"),
                             band.unsqueeze(1).broadcast_to([H, P, BAND])).then_inc(band_written, 16)
                sp.wait_ge(stack_cleared, 1)
                for i in range(2):
                    for e in range(2):
                        for bounce, stack in ((q_bounce[i], q_stack[0:MROWS, 1, :, :]), (k_bounce[i], k_stack[0:MROWS, :, :])):
                            sp.dma_start(bounce[e, MAX_AT:MAX_AT + MROWS, :],
                                         stack.rearrange("r p n -> r (p n)")).then_inc(rows_written, 16)
                sp.wait_ge(rows_written, 128)
                sp.wait_ge(band_written, 16)
                sp.dma_start(bias_whole, bass.AP(tensor=band_bounce.tensor, offset=band_bounce.offset + P - 1,
                                                 ap=[[H * BAND - 1, P], [BAND, H], [1, NEAR]])).then_inc(band_read, 16)

            total_loads = n_loads[0]

            @block.tensor
            def _(pe):
                pe.wait_ge(setup_step, 3)
                nc.tensor.matmul(single[0][0:H, 0:BAND], table[:, :], onehot, start=True, stop=True).then_inc(setup_mm, 1)
                pe.wait_ge(loaded, 16 * total_loads)
                pe.wait_ge(band_read, 16)
                for h in range(0, H, 2):
                    if h >= 2 * RING:
                        pe.wait_ge(bias_copied, h // 2 - RING + 1)
                    for i in range(2):
                        for half in range(2):
                            ins = nc.tensor.transpose(ring[h // 2 % RING][:, 0, NEAR * i + P * half:NEAR * i + P * half + P],
                                                      bias_whole[:, h + i, P * (1 - half):P * (2 - half)], eye[:, :])
                    ins.then_inc(bias_turned, 1)

            @block.vector
            def _(dve):
                nc.vector.memset(table[BUCKETS:BUCKETS + 1, :], MASKED).then_inc(setup_step, 1)
                nc.vector.memset(minus_half[:, :], -0.5).then_inc(setup_step, 1)
                dve.wait_ge(table_loaded, 48)
                nc.vector.tensor_tensor(table[0:BUCKETS, :], table[0:BUCKETS, :], table_far[:, :],
                                        ALU.subtract).then_inc(setup_step, 1)
                dve.wait_ge(setup_mm, 1)
                nc.vector.tensor_copy(band, single[0][0:H, 0:BAND]).then_inc(setup_step, 1)
                dve.wait_ge(loaded, 16 * total_loads)
                nc.vector.tensor_copy(eye_bf[:, :], eye[:, :])
                nc.vector.tensor_copy(mask_kq[:, :], mask_f[:, 0, :])
                nc.vector.tensor_copy(mask_qk[:, :], mask_f[:, 1, :])
                nc.vector.tensor_copy(expert_rows[:, :], expert_rows_f[:, :])
                dve.wait_ge(band_read, 16)
                dve.wait_ge(bias_turned, H // 2)
                n = 4
                nc.vector.tensor_copy(bias_added[:, :, :], bias_whole[:, H - ADDED_HEADS:H, :])
                bias_split = bias_whole[:, 0:H - ADDED_HEADS, :]
                for part in range(3):
                    nc.vector.tensor_copy(bias_kq[:, part, :, :], bias_split).then_inc(setup_step, 1)
                    n += 1
                    if part < 2:
                        dve.wait_ge(setup_step, n)
                        nc.vector.tensor_tensor(bias_split, bias_split, bias_kq[:, part, :, :], ALU.subtract).then_inc(setup_step, 1)
                        n += 1
                        dve.wait_ge(setup_step, n)

            @block.gpsimd
            def _(pool):
                nc.gpsimd.memset(m_parts[:, :, :, :, :], 0.0)
                nc.gpsimd.memset(k_stack[:, :, :], 1.0)
                nc.gpsimd.memset(q_stack[:, :, :, :], 0.0).then_inc(stack_cleared, 1)
                for l in range(2):
                    nc.gpsimd.memset(v_aug[l][:, :, :, :], 0.0).then_inc(pool_step, 1)
                pool.wait_ge(pool_step, 2)
                for l in range(2):
                    nc.gpsimd.memset(v_aug[l][:, :, :, D:D + 1], 1.0)

        nc.all_engine_barrier(sems_to_clear=all_sems)

        def consumed(step):
            kind, a = step[0], step[1:]
            if kind == "max":
                return heads_maxed[a[0]], heads_by(a[1], a[2]) if a[0] == 0 else nth(*step)
            if kind == "exp":
                return exp_done[a[0]], nth(*step)
            if kind == "turn_max":
                return m_in_stack[a[0]], a[1] + 1
            if kind == "context":
                return ctx_ready[a[0]], 2 * a[1] + 2
            if kind in ("up", "widen"):
                return {"up": hidden_ready, "widen": weight_bc_ready}[kind], a[0] + 1
            if kind in ("gate", "turn_weights", "finish"):
                return {"gate": gate_read, "turn_weights": weight_copied, "finish": moe_read}[kind], 1
            return {"context_back": ctx_copied, "attended": y_read, "to_channels": hT_ready, "project_k": k_read,
                    "project_q": q_read, "project_v": v_ready}[kind][a[0]], 1

        def prob_index(l, g, kt, older):
            return NT * g + kt + (GROUPS * NT if l == 0 and older is not None else 0)

        def run(oldest, older, newer):
            steps = body_steps(oldest is not None, older is not None, newer is not None)
            uses = [s for s in steps if s[0] in RING_KINDS]

            def slot_of(step):
                return ring[uses.index(step) % RING]

            with nc.Block() as block:
                @block.sync
                def _(sp):
                    if newer is not None:
                        sp.dma_start(x[:, :, :], din["L0_attn_x"][bass.ds(newer, 1), :, :].rearrange(
                            "a (t p) c -> p (a t) c", p=P)).then_inc(x_loaded, 16)

                    def bounce_out(parts, repeat, split, bounce, bounced):
                        sp.wait_ge(split, 1)
                        for n, row in ((3, 0), (1, 3 * D), (2, MAX_AT + MROWS)):
                            part = 3 - n
                            for e in range(2):
                                half = slice(64 * e, 64 * e + 64)
                                src = parts[half, part:part + 1, :].broadcast_to([64, n, T]) if repeat else parts[half, 0:n, :]
                                dst = bounce[e, row:row + n * D, :].rearrange(
                                    "(s d) (p n) -> (d p) s n", s=n, p=PAIRS)
                                sp.dma_start(dst, src).then_inc(bounced, 16)

                    def split(l, i, stage):
                        if stage < 2:
                            return
                        if i == 0:
                            bounce_out(k_parts, False, k_split[l], k_bounce[l], k_bounced[l])
                        else:
                            bounce_out(q_parts, True, q_split[l], q_bounce[l], q_bounced[l])

                    def groups_in(l, g, n):
                        if g == 0:
                            sp.wait_ge(k_bounced[l], 16 * 6)
                            sp.wait_ge(q_bounced[l], 16 * 6)
                        if l == 0 and older is not None:
                            sp.wait_ge(exp_scores[1], nth("exp", 1, g, len(EXP_PIECES) - 1))
                        for e in range(2):
                            pairs = slice(GP * g, GP * (g + n))
                            for stack, bounce in ((k_stack[:, pairs, :], k_bounce[l]), (q_stack[:, e, pairs, :], q_bounce[l])):
                                sp.dma_start(stack[64 * e:64 * e + STACK, :, :].rearrange("r p n -> r (p n)"),
                                             bounce[e, :, GP * T * g:GP * T * (g + n)]).then_inc(stack_in[l][g], 16)

                    for s in steps:
                        if s[0] == "split":
                            split(*s[1:])
                        elif s[0] == "stack_in":
                            groups_in(*s[1:])
                    if newer is not None:
                        sp.wait_ge(stack_in[1][0], 64)
                    if oldest is not None:
                        sp.wait_ge(result_ready, NT)
                        sp.dma_start(out[bass.ds(oldest, 1), :, :].rearrange("a (t p) c -> p (a t) c", p=P),
                                     result[:, :, :]).then_inc(stored, 16)
                        sp.wait_ge(stored, 16)

                @block.tensor
                def _(pe):
                    mm = nc.tensor.matmul

                    def claim(step):
                        i = uses.index(step)
                        if i >= RING:
                            pe.wait_ge(*consumed(uses[i - RING]))
                        return ring[i % RING]

                    def to_channels(slot, l):
                        pe.wait_ge(normed_ready[l], NT)
                        for t in range(NT):
                            ins = nc.tensor.transpose(slot[:, 0, P * t:P * t + P], normed[l // 2][:, t, :], eye[:, :])
                        ins.then_inc(normed_turned[l], 1)

                    def project_k(slot, l):
                        pe.wait_ge(hT_ready[l], 1)
                        ins = mm(slot[:, 0, :], wk[l][:, :], hT[0][:, :], start=True, stop=True)
                        if l == 0:
                            ins = mm(slot[:, 1, :], wk_rot[:, :], hT[0][:, :], start=True, stop=True)
                        ins.then_inc(k_proj[l], 1)

                    def project_q(slot, l):
                        ins = mm(slot[:, 0, :], wq[l][:, :], hT[0][:, :], start=True, stop=True)
                        if l == 0:
                            ins = mm(slot[:, 1, :], wq_rot[:, :], hT[0][:, :], start=True, stop=True)
                        ins.then_inc(q_proj[l], 1)

                    def project_v(slot, l):
                        for t in range(NT):
                            ins = mm(slot[:, 0, P * t:P * t + P], hT[0][:, P * t:P * t + P], wv[l][:, :], start=True, stop=True)
                        ins.then_inc(v_proj[l], 1)

                    def max_piece(slot, l, g, n):
                        if l == 0 and n == 0:
                            pe.wait_ge(stack_in[0][g], 64)
                        tile, pair0, pairs = MAX_PIECES[n]
                        keys = P * (tile + 1)
                        for pr in range(pairs):
                            pair = GP * g + pair0 + pr
                            for e in range(2):
                                ins = mm(slot[:, e, keys * pr:keys * (pr + 1)],
                                         q_stack[:, e, pair, P * tile:P * tile + P], k_stack[:, pair, 0:keys],
                                         start=True, stop=(l == 0))
                            if l == 1:
                                for e in range(2):
                                    ins = mm(slot[:, e, keys * (pr + 1) - P:keys * (pr + 1)], eye_bf[:, :],
                                             mask_qk[:, :], start=False, stop=True)
                        ins.then_inc(max_scores[l], 1)

                    def turn_max(slot, l, g):
                        pe.wait_ge(m_split[l], g + 1)
                        view = slot[:, 0, :].bitcast(BF16).rearrange("p (r n) -> p r n", r=GP)
                        for t in range(NT):
                            for r in range(GP):
                                ins = nc.tensor.transpose(view[:, r, P * t:P * t + P], m_parts[:, g % 2, t, r, :], eye_bf[:, :])
                        ins.then_inc(m_turned[l], 1)

                    def exp_piece(slot, l, g, n):
                        tile, pair0, pairs = EXP_PIECES[n]
                        queries = T - P * tile
                        near = min(NEAR, queries)
                        if n == 0:
                            pe.wait_ge(m_in_stack[l], g + 1)
                        for pr in range(pairs):
                            pair = GP * g + pair0 + pr
                            for e in range(2):
                                ins = mm(slot[:, e, queries * pr:queries * (pr + 1)],
                                         k_stack[:, pair, P * tile:P * tile + P], q_stack[:, e, pair, P * tile:T],
                                         start=True, stop=(l == 0 and g >= ADD_FROM))
                            for e in range(2):
                                if l == 0 and g >= ADD_FROM:
                                    continue
                                if l == 0:
                                    for part in range(3):
                                        ins = mm(slot[:, e, queries * pr:queries * pr + near], eye_bf[:, :],
                                                 bias_kq[:, part, 2 * pair + e, 0:near], start=False, stop=(part == 2))
                                else:
                                    ins = mm(slot[:, e, queries * pr:queries * pr + P], eye_bf[:, :], mask_kq[:, :],
                                             start=False, stop=True)
                        ins.then_inc(exp_scores[l], 1)

                    def values(l, g, kt):
                        acc = single[g % 2]
                        last = {0: 1, 1: 3, 2: 4, 3: 5}[kt]
                        pe.wait_ge(exp_done[l], nth("exp", l, g, last))
                        if kt == 0 and g >= 2:
                            pe.wait_ge(ctxT_copied[l], g - 1)
                        elif kt == 0 and l == 0 and older is not None:
                            pe.wait_ge(ctxT_copied[1], g + 3)
                        queries = T - P * kt
                        for j in range(GH):
                            ins = mm(acc[VCOL * j:VCOL * j + VCOL, P * kt:T], v_aug[l][:, kt, GH * g + j, :],
                                     probs[:, prob_index(l, g, kt, older) % PBUF, j, 0:queries], start=(kt == 0), stop=(kt == NT - 1))
                        ins.then_inc(values_done[l], 1)

                    def context(slot, l, k):
                        pe.wait_ge(ctxT_copied[l], GROUPS)
                        for i in range(2):
                            t = 2 * k + i
                            for g in range(GROUPS):
                                ins = nc.tensor.transpose(slot[:, i, P * g:P * g + P], ctxT[:, g, P * t:P * t + P], eye[:, :])
                            ins.then_inc(ctx_turned[l], 1)

                    def context_back(slot, l):
                        for t in range(NT):
                            pe.wait_ge(ctx_ready[l], t + 1)
                            ins = nc.tensor.transpose(slot[:, 0, P * t:P * t + P], ctx_tok[:, t, :], eye[:, :])
                        ins.then_inc(ctx_back[l], 1)

                    def attended(slot, l):
                        pe.wait_ge(ctx_copied[l], 1)
                        for t in range(NT):
                            ins = mm(slot[:, 0, P * t:P * t + P], ctx_ch[:, P * t:P * t + P], wo[l][:, :], start=True, stop=True)
                        ins.then_inc(y_ready[l], 1)

                    def gate_scores(slot):
                        pe.wait_ge(hT_ready[2], 1)
                        for t in range(NT):
                            ins = mm(slot[:, 0, EXPERTS * t:EXPERTS * t + EXPERTS], hT[1][:, P * t:P * t + P], gate[:, :],
                                     start=True, stop=True)
                        ins.then_inc(gate_ready, 1)

                    def turn_weights(slot):
                        pe.wait_ge(weight_split, 1)
                        view = slot[:, 0, :].bitcast(BF16)
                        for t in range(NT):
                            ins = nc.tensor.transpose(view[0:3 * EXPERTS, P * t:P * t + P],
                                                      weight_parts[:, t, :, :].rearrange("p s e -> p (s e)"), eye_bf[:, :])
                        ins.then_inc(weight_turned, 1)

                    def up(slot, i):
                        e, a = i // HALVES, i % HALVES
                        mm(slot[:, 0, :], w1[:, e, P * a:P * a + P], hT[1][:, :], start=True, stop=True)
                        mm(slot[:, 1, :], w2[:, e, P * a:P * a + P], hT[1][:, :], start=True, stop=True).then_inc(up_ready, 1)

                    def widen(slot, e):
                        if e == 0:
                            pe.wait_ge(weight_copied, 1)
                        mm(slot[:, 0, :], expert_rows[:, P * e:P * e + P], weight_rows[:, :], start=True,
                           stop=True).then_inc(weight_wide, 1)

                    def down(i):
                        e, a = i // HALVES, i % HALVES
                        if i == 0 and newer is not None:
                            pe.wait_ge(ctxT_copied[0], GROUPS)
                        pe.wait_ge(hidden_w_ready, i + 1)
                        mm(single[0][:, :], w3[:, e, a, :], hidden_w[:, i % EBUF, :], start=(i == 0),
                           stop=(i == UNITS - 1)).then_inc(down_done, 1)

                    def finish(slot):
                        for t in range(NT):
                            ins = nc.tensor.transpose(slot[:, 0, P * t:P * t + P], moe_ch[:, P * t:P * t + P], eye[:, :])
                        ins.then_inc(moe_turned, 1)

                    parts = {"to_channels": to_channels, "project_k": project_k, "project_q": project_q, "project_v": project_v,
                             "max": max_piece, "turn_max": turn_max, "exp": exp_piece, "values": values, "context": context,
                             "context_back": context_back, "attended": attended, "gate": gate_scores,
                             "turn_weights": turn_weights, "up": up, "widen": widen, "down": down, "finish": finish}
                    for s in steps:
                        if s[0] in RING_KINDS:
                            parts[s[0]](claim(s), *s[1:])
                        elif s[0] in parts:
                            parts[s[0]](*s[1:])

                @block.scalar
                def _(act):
                    def to_channels(slot, l):
                        act.wait_ge(normed_turned[l], 1)
                        if l == 0:
                            nc.scalar.activation(hT[0][:, :], slot[:, 0, :], ACT.Copy).then_inc(hT_ready[0], 1)
                        else:
                            col = 2 * (l - 1)
                            nc.scalar.activation(hT[l - 1][:, :], slot[:, 0, :], ACT.Identity, bias=ln_cols[:, col + 1:col + 2],
                                                 scale=ln_cols[:, col:col + 1]).then_inc(hT_ready[l], 1)

                    def project_k(slot, l):
                        if l == 1:
                            act.wait_ge(k_proj[1], 1)
                            nc.scalar.activation(qk_f[:, 0, :], slot[:, 0, :], ACT.Copy).then_inc(k_read[1], 1)

                    def project_q(slot, l):
                        if l == 1:
                            act.wait_ge(q_proj[1], 1)
                            nc.scalar.activation(qk_f[:, 1, :], slot[:, 0, :], ACT.Copy).then_inc(q_read[1], 1)

                    def split(l, i, stage):
                        parts, rounded = ((k_parts, k_rounded), (q_parts, q_rounded))[i]
                        if stage == 0:
                            if l == 0:
                                act.wait_ge((k_summed, q_summed)[i], 1)
                            else:
                                act.wait_ge((k_read, q_read)[i][1], 1)
                                if newer is not None:
                                    act.wait_ge((k_bounced, q_bounced)[i][0], 96)
                            nc.scalar.activation(parts[:, 0, :], qk_f[:, i, :], ACT.Copy).then_inc(rounded[l], 1)
                        if stage == 1:
                            act.wait_ge((k_rest_ready, q_rest_ready)[i][l], 1)
                            nc.scalar.activation(parts[:, 1, :], qk_rest[:, i, :], ACT.Copy).then_inc(rounded[l], 1)

                    def turn_max(slot, l, g):
                        act.wait_ge(m_turned[l], g + 1)
                        view = slot[:, 0, :].bitcast(BF16).rearrange("p (r n) -> p r n", r=GP)
                        for e in range(2):
                            rows = slice(64 * e + MAX_AT, 64 * e + MAX_AT + MROWS)
                            ins = nc.scalar.activation(q_stack[rows, e, GP * g:GP * g + GP, :], view[rows, :, :], ACT.Copy)
                        ins.then_inc(m_in_stack[l], 1)

                    def exp_piece(slot, l, g, i):
                        tile, pair0, pairs = EXP_PIECES[i]
                        queries = T - P * tile
                        buf = probs[:, prob_index(l, g, tile, older) % PBUF, :, :]
                        if l == 0 and g >= ADD_FROM:
                            act.wait_ge(bias_in, nth("exp", l, g, i) - nth("exp", l, ADD_FROM, 0) + 1)
                        else:
                            act.wait_ge(exp_scores[l], nth("exp", l, g, i))
                        before = prob_index(l, g, tile, older) - PBUF
                        if pair0 == 0 and before >= 0:
                            layer = 1 if l == 0 and older is not None and before < GROUPS * NT else l
                            before %= GROUPS * NT
                            act.wait_ge(values_done[layer], nth("values", layer, before // NT, before % NT))
                        src = slot[:, :, 0:queries * pairs].rearrange("p e (r q) -> p e r q", r=pairs)
                        dst = buf[:, 2 * pair0:2 * pair0 + 2 * pairs, 0:queries].rearrange("p (r e) q -> p e r q", e=2)
                        if pairs == 1:
                            src, dst = src[:, :, 0, :], dst[:, :, 0, :]
                        nc.scalar.activation(dst, src, ACT.Exp, scale=SCALE).then_inc(exp_done[l], 1)

                    def values(l, g, kt):
                        if kt == NT - 1:
                            if g == 0 and l == 0 and older is not None:
                                act.wait_ge(ctx_turned[1], NT)
                            act.wait_ge(values_done[l], nth("values", l, g, kt))
                            nc.scalar.activation(ctxT[:, g, :], single[g % 2][:, :], ACT.Copy).then_inc(ctxT_copied[l], 1)

                    def context_back(slot, l):
                        act.wait_ge(ctx_back[l], 1)
                        nc.scalar.activation(ctx_ch[:, :], slot[:, 0, :], ACT.Copy).then_inc(ctx_copied[l], 1)

                    def gate_scores(slot):
                        act.wait_ge(gap_ready, 1)
                        nc.scalar.activation(gap_exp[:, :], gap[:, :], ACT.Exp).then_inc(gap_exp_ready, 1)

                    def turn_weights(slot):
                        act.wait_ge(weight_turned, 1)
                        nc.scalar.activation(weight_rows[:, :], slot[:, 0, :].bitcast(BF16)[0:3 * EXPERTS, 0:T],
                                             ACT.Copy).then_inc(weight_copied, 1)

                    def up(slot, i):
                        act.wait_ge(up_ready, i + 1)
                        if i >= EBUF:
                            act.wait_ge(gated_ready, i - EBUF + 1)
                        nc.scalar.activation(tanh_t[:, i % EBUF, :], slot[:, 0, :], ACT.Tanh, scale=0.5).then_inc(tanh_ready, 1)

                    def widen(slot, e):
                        act.wait_ge(weight_wide, e + 1)
                        if e >= 2:
                            act.wait_ge(hidden_w_ready, HALVES * (e - 1))
                        nc.scalar.activation(weight_bc[:, e % 2, :], slot[:, 0, :], ACT.Copy, scale=0.5).then_inc(weight_bc_ready, 1)

                    def keep_x1():
                        if oldest is not None:
                            act.wait_ge(result_ready, NT)
                        nc.scalar.activation(x1_older[:, :, :], x1[:, :, :], ACT.Copy).then_inc(x1_kept, 1)

                    def keep_experts():
                        if oldest is not None:
                            act.wait_ge(moe_turned, 1)
                        act.wait_ge(down_done, UNITS)
                        nc.scalar.activation(moe_ch[:, :], single[0][:, :], ACT.Copy).then_inc(moe_copied, 1)

                    parts = {"to_channels": to_channels, "project_k": project_k, "project_q": project_q, "split": split, "turn_max": turn_max,
                             "exp": exp_piece, "values": values, "context_back": context_back, "gate": gate_scores,
                             "turn_weights": turn_weights, "up": up, "widen": widen, "keep_x1": keep_x1,
                             "keep_experts": keep_experts}
                    for s in steps:
                        if s[0] in parts:
                            parts[s[0]](*([slot_of(s)] if s[0] in RING_KINDS else []), *s[1:])

                def split3(engine, whole, rest, parts, step, last):
                    step(engine.tensor_copy(parts[0], whole))
                    step(engine.tensor_tensor(rest, whole, parts[0], ALU.subtract))
                    step(engine.tensor_copy(parts[1], rest))
                    engine.tensor_tensor(parts[2], rest, parts[1], ALU.subtract).then_inc(last, 1)

                def subtract_parts(queue, engine, l, i, stage):
                    parts, rounded = ((k_parts, k_rounded), (q_parts, q_rounded))[i]
                    if stage == 0 and l == 0:
                        queue.wait_ge((k_read, q_read)[i][0], 1)
                        engine.tensor_tensor(qk_f[:, i, :], rope_a[:, i, :], rope_b[:, i, :],
                                             ALU.add).then_inc((k_summed, q_summed)[i], 1)
                    if stage == 1:
                        queue.wait_ge(rounded[l], 1)
                        engine.tensor_tensor(qk_rest[:, i, :], qk_f[:, i, :], parts[:, 0, :],
                                             ALU.subtract).then_inc((k_rest_ready, q_rest_ready)[i][l], 1)
                    if stage == 2:
                        queue.wait_ge(rounded[l], 2)
                        engine.tensor_tensor(parts[:, 2, :], qk_rest[:, i, :], parts[:, 1, :],
                                             ALU.subtract).then_inc((k_split, q_split)[i][l], 1)

                @block.gpsimd
                def _(pool):
                    steps_done = [0]

                    def step(ins):
                        steps_done[0] += 1
                        ins.then_inc(pool_step, 1)
                        pool.wait_ge(pool_step, steps_done[0])

                    def stats(n):
                        pool.wait_ge(var_ready[n], 1)
                        nc.gpsimd.tensor_tensor(rstd[:, n, :], var_eps[:, n, :], minus_half[:, :], ALU.pow).then_inc(rstd_ready[n], 1)

                    def split(l, i, stage):
                        if l == 0:
                            subtract_parts(pool, nc.gpsimd, l, i, stage)

                    def turn_max(l, g):
                        pool.wait_ge(group_max[l], g + 1) if l == 0 else pool.wait_ge(heads_maxed[1], nth("max", 1, g, 5))
                        if g >= 2:
                            pool.wait_ge(m_turned[l], g - 1)
                        elif l == 0 and older is not None:
                            pool.wait_ge(m_turned[1], g + 3)
                        by_half = m_parts[:, g % 2, :, :, :].rearrange("p t r (e c) -> p t r e c", e=2)
                        shape = lambda i: by_half[:, :, :, :, MAX_AT + i]
                        view = lambda m: m[:, g, :, :].rearrange("p t (r e) -> p t r e", e=2)
                        split3(nc.gpsimd, view(neg_max), view(m_rest), [shape(i) for i in range(3)], step, m_split[l])

                    def up(i):
                        pool.wait_ge(hidden_ready, i + 1)
                        pool.wait_ge(weight_bc_ready, i // HALVES + 1)
                        if i >= EBUF:
                            pool.wait_ge(down_done, i - EBUF + 1)
                        nc.gpsimd.tensor_tensor(hidden_w[:, i % EBUF, :], hidden[:, i % EBUF, :],
                                                weight_bc[:, (i // HALVES) % 2, :], ALU.mult).then_inc(hidden_w_ready, 1)

                    parts = {"stats": stats, "split": split, "turn_max": turn_max, "up": up}
                    for s in steps:
                        if s[0] in parts:
                            parts[s[0]](*s[1:])

                @block.vector
                def _(dve):
                    steps_done, nears = [0], [0]

                    def step(ins):
                        steps_done[0] += 1
                        ins.then_inc(vector_step, 1)
                        dve.wait_ge(vector_step, steps_done[0])

                    normed_by = {0: (x, None, 0), 1: (branch, x1, None), 2: (x1, u, None), 3: (u, None, 1),
                                 4: (u2, None, 2), 5: (branch, result, None)}

                    def stats(n):
                        src = normed_by[n][0]
                        if n == 0:
                            dve.wait_ge(x_loaded, 16)
                        if n == 1 and older is not None:
                            dve.wait_ge(x1_kept, 1)
                        for t in range(NT):
                            ins = nc.vector.bn_stats(stats_t[:, t, :], src[:, t, :])
                        step(ins)
                        for t in range(NT):
                            ins = nc.vector.bn_aggr(mean_var[:, n, t, :], stats_t[:, t, :])
                        step(ins)
                        nc.vector.tensor_scalar(var_eps[:, n, :], mean_var[:, n, :, 1], EPS, None, ALU.add).then_inc(var_ready[n], 1)

                    def norm(n):
                        src, dst, stage = normed_by[n]
                        if stage is not None:
                            dst = normed[stage // 2]
                        dve.wait_ge(rstd_ready[n], 1)
                        for t in range(NT):
                            ins = nc.vector.tensor_scalar(dst[:, t, :], src[:, t, :], mean_var[:, n, t, 0:1], rstd[:, n, t:t + 1],
                                                          ALU.subtract, ALU.mult)
                            if stage is not None:
                                ins.then_inc(normed_ready[stage], 1)
                        if stage is None:
                            step(ins)
                        if n == 1:
                            step(nc.vector.tensor_tensor(x1[:, :, :], x1[:, :, :], x[:, :, :], ALU.add))
                        if n == 5:
                            for t in range(NT):
                                nc.vector.tensor_tensor(result[:, t, :], result[:, t, :], x1_older[:, t, :], ALU.add).then_inc(result_ready, 1)

                    def project(i, slot, proj, read):
                        col = 2 - 2 * i
                        dve.wait_ge(proj, 1)
                        nc.vector.scalar_tensor_tensor(rope_a[:, i, :], slot[:, 0, :], bias_cols[:, col:col + 1], cos_t[:, :],
                                                       ALU.add, ALU.mult)
                        nc.vector.scalar_tensor_tensor(rope_b[:, i, :], slot[:, 1, :], bias_cols[:, col + 1:col + 2],
                                                       sin_t[:, :], ALU.add, ALU.mult).then_inc(read, 1)

                    def project_k(slot, l):
                        if l == 0:
                            project(0, slot, k_proj[0], k_read[0])

                    def project_q(slot, l):
                        if l == 0:
                            project(1, slot, q_proj[0], q_read[0])

                    def project_v(slot, l):
                        dve.wait_ge(v_proj[l], 1)
                        src = slot[:, 0, :].rearrange("p (t h d) -> p t h d", t=NT, h=H)
                        for t in range(NT):
                            if l == 0:
                                ins = nc.vector.tensor_tensor(v_aug[l][:, t, :, 0:D], src[:, t, :, :],
                                                              bv_row[:, :].rearrange("p (h d) -> p h d", h=H), ALU.add)
                            else:
                                ins = nc.vector.tensor_copy(v_aug[l][:, t, :, 0:D], src[:, t, :, :])
                        ins.then_inc(v_ready[l], 1)

                    def split(l, i, stage):
                        if l == 1:
                            subtract_parts(dve, nc.vector, l, i, stage)

                    def max_piece(slot, l, g, n):
                        tile, pair0, pairs = MAX_PIECES[n]
                        keys = P * (tile + 1)
                        heads = 2 * pairs
                        h0 = GH * g + 2 * pair0
                        dve.wait_ge(max_scores[l], nth("max", l, g, n))
                        if l == 0 and n == 0 and older is not None:
                            dve.wait_ge(m_split[1], g + 1)
                        scores = slot[:, :, 0:keys * pairs].rearrange("p e (r k) -> p e r k", r=pairs)
                        if pairs == 1:
                            scores = scores[:, :, 0, :]
                        if l == 1:
                            dst = neg_max[:, g, tile, 2 * pair0:2 * pair0 + heads].rearrange("p (r e) -> p e r", e=2)
                            if pairs == 1:
                                dst = dst[:, :, 0]
                            nc.vector.tensor_reduce(dst, scores, AX_X, ALU.max, negate=True).then_inc(heads_maxed[1], 1)
                            return
                        if tile >= 2:
                            nc.vector.tensor_reduce(far_max[:, tile, h0:h0 + heads], scores[:, :, 0:keys - NEAR], AX_X, ALU.max)
                        near = min(NEAR, keys)
                        for r in range(pairs):
                            for e in range(2):
                                h = h0 + 2 * r + e
                                if nears[0] >= NBUF:
                                    dve.wait_ge(heads_maxed[0], nears[0] - NBUF + 1)
                                nc.vector.tensor_tensor_reduce(
                                    out=near_sum[:, nears[0] % NBUF, 0:near], in0=slot[:, e, keys * (r + 1) - near:keys * (r + 1)],
                                    in1=bias_qk[:, h, NEAR - near:NEAR], scale=1.0, scalar=2.0 * MASKED, op0=ALU.add, op1=ALU.max,
                                    accum_out=near_max[:, tile, h:h + 1]).then_inc(heads_maxed[0], 1)
                                nears[0] += 1
                        if n == len(MAX_PIECES) - 1:
                            dve.wait_ge(heads_maxed[0], nears[0])
                            hs = slice(GH * g, GH * g + GH)
                            nc.vector.tensor_scalar(neg_max[:, g, 0:2, :], near_max[:, 0:2, hs], -1.0, None, ALU.mult)
                            step(nc.vector.tensor_tensor(m_most[:, g, 2:NT, :], near_max[:, 2:NT, hs], far_max[:, 2:NT, hs], ALU.max))
                            nc.vector.tensor_scalar(neg_max[:, g, 2:NT, :], m_most[:, g, 2:NT, :], -1.0, None,
                                                    ALU.mult).then_inc(group_max[l], 1)

                    def exp_piece(slot, l, g, n):
                        if l == 1 or g < ADD_FROM:
                            return
                        tile, pair0, pairs = EXP_PIECES[n]
                        queries = T - P * tile
                        near = min(NEAR, queries)
                        h0 = GH * (g - ADD_FROM) + 2 * pair0
                        scores = slot[:, :, 0:queries * pairs].rearrange("p e (r q) -> p e r q", r=pairs)[:, :, :, 0:near]
                        bias = bias_added[:, h0:h0 + 2 * pairs, 0:near].rearrange("p (r e) q -> p e r q", e=2)
                        if pairs == 1:
                            scores, bias = scores[:, :, 0, :], bias[:, :, 0, :]
                        dve.wait_ge(exp_scores[0], nth("exp", l, g, n))
                        nc.vector.tensor_tensor(scores, scores, bias, ALU.add).then_inc(bias_in, 1)

                    def context(slot, l, k):
                        for i in range(2):
                            t = 2 * k + i
                            dve.wait_ge(ctx_turned[l], t + 1)
                            src = slot[:, i, :].rearrange("p (h v) -> p h v", h=H)
                            step(nc.vector.reciprocal(row_inv[:, t, :], src[:, :, D]))
                            nc.vector.tensor_tensor(ctx_tok[:, t, :].rearrange("p (h d) -> p h d", h=H), src[:, :, 0:D],
                                                    row_inv[:, t, :].unsqueeze(2).broadcast_to([P, H, D]),
                                                    ALU.mult).then_inc(ctx_ready[l], 1)

                    def attended(slot, l):
                        dve.wait_ge(y_ready[l], 1)
                        dst = branch if l == 0 else u2
                        nc.vector.tensor_tensor(dst[:, :, :], slot[:, 0, :].rearrange("p (t c) -> p t c", t=NT),
                                                bo_row[l][:, :].unsqueeze(1).broadcast_to([P, NT, C]), ALU.add).then_inc(y_read[l], 1)
                        dve.wait_ge(y_read[l], 1)
                        if l == 1:
                            step(nc.vector.tensor_tensor(u2[:, :, :], u2[:, :, :], u[:, :, :], ALU.add))

                    def gate_scores(slot):
                        dve.wait_ge(gate_ready, 1)
                        nc.vector.tensor_copy(gate_s[:, :, :], slot[:, 0, 0:NT * EXPERTS].rearrange(
                            "p (t e) -> p t e", t=NT)).then_inc(gate_read, 1)
                        dve.wait_ge(gate_read, 1)
                        for t in range(NT):
                            ins = nc.vector.max(top8[:, t, :], gate_s[:, t, :])
                        step(ins)
                        nc.vector.tensor_tensor(gap[:, :], top8[:, :, 1], top8[:, :, 0], ALU.subtract).then_inc(gap_ready, 1)
                        for t in range(NT):
                            ins = nc.vector.max_index(top_ids[:, t, :], top8[:, t, :], gate_s[:, t, :])
                        step(ins)
                        step(nc.vector.tensor_copy(top_ids_f[:, :, :], top_ids[:, :, 0:2]))

                    def weigh():
                        dve.wait_ge(gap_exp_ready, 1)
                        step(nc.vector.tensor_scalar(gap_den[:, :], gap_exp[:, :], 1.0, None, ALU.add))
                        step(nc.vector.reciprocal(top_p[:, 0, :], gap_den[:, :]))
                        step(nc.vector.tensor_tensor(top_p[:, 1, :], top_p[:, 0, :], gap_exp[:, :], ALU.mult))
                        for k in range(2):
                            ins = nc.vector.tensor_tensor(pick[:, k, :, :], expert_ids[:, :, :],
                                                          top_ids_f[:, :, k].unsqueeze(2).broadcast_to([P, NT, EXPERTS]), ALU.is_equal)
                        step(ins)
                        for k in range(2):
                            ins = nc.vector.tensor_tensor(pick_w[:, k, :, :], pick[:, k, :, :],
                                                          top_p[:, k, :].unsqueeze(2).broadcast_to([P, NT, EXPERTS]), ALU.mult)
                        step(ins)
                        step(nc.vector.tensor_tensor(weight[:, :, :], pick_w[:, 0, :, :], pick_w[:, 1, :, :], ALU.add))
                        split3(nc.vector, weight[:, :, :], weight_rest[:, 0, :, :],
                               [weight_parts[:, :, i, :] for i in range(3)], step, weight_split)

                    def up(slot, i):
                        dve.wait_ge(tanh_ready, i + 1)
                        nc.vector.scalar_tensor_tensor(gated[:, i % EBUF, :], tanh_t[:, i % EBUF, :], 1.0, slot[:, 0, :],
                                                       ALU.add, ALU.mult).then_inc(gated_ready, 1)
                        dve.wait_ge(gated_ready, i + 1)
                        if i >= EBUF:
                            dve.wait_ge(hidden_w_ready, i - EBUF + 1)
                        nc.vector.tensor_tensor(hidden[:, i % EBUF, :], gated[:, i % EBUF, :], slot[:, 1, :],
                                                ALU.mult).then_inc(hidden_ready, 1)

                    def finish(slot):
                        dve.wait_ge(moe_turned, 1)
                        nc.vector.tensor_tensor(branch[:, :, :], u2[:, :, :], slot[:, 0, :].rearrange("p (t c) -> p t c", t=NT),
                                                ALU.add).then_inc(moe_read, 1)
                        dve.wait_ge(moe_read, 1)

                    parts = {"stats": stats, "norm": norm, "project_k": project_k, "project_q": project_q, "project_v": project_v,
                             "split": split, "max": max_piece, "exp": exp_piece, "context": context, "attended": attended,
                             "gate": gate_scores, "weigh": weigh, "up": up, "finish": finish}
                    for s in steps:
                        if s[0] in parts:
                            parts[s[0]](*([slot_of(s)] if s[0] in RING_KINDS else []), *s[1:])

            nc.all_engine_barrier(sems_to_clear=all_sems)

        run(None, None, 0)
        run(None, 0, 1)
        with nc.Fori(1, B - 1) as b:
            run(b - 1, b, b + 1)
        run(B - 2, B - 1, None)
        run(B - 1, None, None)


AS_GIVEN = ["L0_attn_x", "L0_attn_Wv", "L0_attn_bv", "L0_attn_Wp", "L0_attn_bp", "L0_attn_rel_bias_table",
            "L0_ffn_ln1_scale", "L0_ffn_ln1_shift", "L0_ffn_wv", "L0_ffn_wo", "L0_ffn_bo", "L0_ffn_ln2_scale",
            "L0_ffn_ln2_shift", "L0_ffn_gate_w", "L0_ffn_w1", "L0_ffn_w2", "L0_ffn_w3"]


def by_parity(w, partner=False):
    w = np.asarray(w)
    w = w.reshape(w.shape[:-1] + (PAIRS, 2, D))
    if partner:
        w = np.concatenate([w[..., D // 2:], w[..., :D // 2]], axis=-1)
    return np.moveaxis(w, -3, -1).reshape(w.shape[:-3] + (C,))


def kernel(**inputs):
    import concourse.bacc as bacc
    from concourse.bass_utils import run_bass_kernel_spmd

    laid_out = {name: inputs[name] for name in AS_GIVEN}
    laid_out["qk_weights"] = np.stack([
        by_parity(inputs["L0_attn_Wq"]), by_parity(inputs["L0_attn_Wk"]),
        by_parity(inputs["L0_ffn_wq"]), by_parity(inputs["L0_ffn_wk"]),
        by_parity(inputs["L0_attn_Wq"], True), by_parity(inputs["L0_attn_Wk"], True)])
    laid_out["qk_biases"] = np.stack([
        by_parity(inputs["L0_attn_bq"]), by_parity(inputs["L0_attn_bq"], True),
        by_parity(inputs["L0_attn_bk"]), by_parity(inputs["L0_attn_bk"], True)], axis=1)
    nc = bacc.Bacc("TRN2", target_bir_lowering=False, num_devices=1)
    arrays, din, const = {}, {}, {}
    for name, a in laid_out.items():
        a = np.ascontiguousarray(a)
        arrays[f"in_{name}"] = a
        din[name] = nc.dram_tensor(f"in_{name}", a.shape, mybir.dt.from_np(a.dtype), kind="ExternalInput").ap()
    for name, a in shape_constants().items():
        arrays[f"const_{name}"] = a
        const[name] = nc.dram_tensor(f"const_{name}", a.shape, F32, kind="ExternalInput").ap()
    out = nc.dram_tensor("out", (B, T, C), F32, kind="ExternalOutput").ap()
    sandwich(nc, din, const, out)
    r = run_bass_kernel_spmd(nc, [arrays], core_ids=[0])
    return r.results[0]["out"]
```
